# Optimizing a Trainium2 kernel written in Bass

```python
import numpy as np
import jax
import jax.numpy as jnp

def _softmax(x, axis=-1):
    return jax.nn.softmax(x, axis=axis)

def _gelu(x):
    return jax.nn.gelu(x, approximate=True)

def _silu(x):
    return jax.nn.silu(x)

def _sigmoid(x):
    return jax.nn.sigmoid(x)

def _layernorm(x, axis=-1, eps=1e-05):
    m = jnp.mean(x, axis=axis, keepdims=True)
    v = jnp.var(x, axis=axis, keepdims=True)
    return (x - m) / jnp.sqrt(v + eps)

def _scatter_add(tgt, idx, src, axis=0):
    return tgt.at[idx].add(src)

def _segment_sum(src, seg, n):
    return jax.ops.segment_sum(src, seg, n)
kernel_name = 'mk_sandwich_d1_jaxref_r8_601e3f'

def setup_inputs(seed: int=0):
    np.random.seed(seed)
    _w = jnp.asarray

    def _L0_attn_setup():
        import jax, jax.numpy as jnp
        import numpy as np
        import math
        N_HEADS = 32
        N_GROUPS = 8
        D_HEAD = 64
        D_MODEL = 256

        def _rope(x):
            S, D = (x.shape[-2], x.shape[-1])
            inv_freq = 1.0 / 10000.0 ** (jnp.arange(0, D, 2, dtype=jnp.float32) / D)
            freqs = jnp.arange(S, dtype=jnp.float32)[:, None] * inv_freq[None, :]
            cos = jnp.repeat(jnp.cos(freqs), 2, axis=-1)
            sin = jnp.repeat(jnp.sin(freqs), 2, axis=-1)
            x2 = x.reshape(*x.shape[:-1], D // 2, 2)
            rot = jnp.stack([-x2[..., 1], x2[..., 0]], axis=-1).reshape(x.shape)
            return x * cos + rot * sin
        key = jax.random.key(seed)
        ks = jax.random.split(key, 6)
        hidden_states = jax.random.normal(ks[0], (2, 256, D_MODEL), dtype=jnp.float32)
        s = 0.02
        Wq = jax.random.normal(ks[1], (D_MODEL, N_HEADS * D_HEAD), dtype=jnp.float32) * s
        Wk = jax.random.normal(ks[2], (D_MODEL, N_GROUPS * D_HEAD), dtype=jnp.float32) * s
        Wv = jax.random.normal(ks[3], (D_MODEL, N_GROUPS * D_HEAD), dtype=jnp.float32) * s
        Wo = jax.random.normal(ks[4], (N_HEADS * D_HEAD, D_MODEL), dtype=jnp.float32) * s
        bo = jnp.zeros((D_MODEL,), dtype=jnp.float32)
        return {'hidden_states': hidden_states, 'Wq': Wq, 'Wk': Wk, 'Wv': Wv, 'Wo': Wo, 'bo': bo}
    _L0_attn_in = _L0_attn_setup()

    def _L0_ffn_setup():
        import jax, jax.numpy as jnp
        import numpy as np
        E = 8
        TOP_K = 2
        H = 256
        I_MOE = 176
        I_SH = 704
        B, S = (2, 256)

        def _moe_forward(hidden_states, router_weight, gate_up_proj, down_proj, sh_gate_w, sh_up_w, sh_down_w, shared_gate_w):
            b, s, h = hidden_states.shape
            x = hidden_states.reshape(-1, h)
            shared = jnp.einsum('ti,hi->th', jax.nn.silu(x @ sh_gate_w.T) * (x @ sh_up_w.T), sh_down_w)
            logits = x @ router_weight.T
            probs = jax.nn.softmax(logits.astype(jnp.float32), axis=-1)
            top_v, top_i = jax.lax.top_k(probs, TOP_K)
            top_v = top_v / top_v.sum(axis=-1, keepdims=True)
            combine = (jax.nn.one_hot(top_i, E, dtype=top_v.dtype) * top_v[..., None]).sum(axis=1)
            out = jnp.zeros_like(x)
            for e in range(E):
                gu = x @ gate_up_proj[e].T
                gate, up = (gu[:, :I_MOE], gu[:, I_MOE:])
                cur = jax.nn.silu(gate) * up @ down_proj[e].T
                out = out + cur * combine[:, e:e + 1]
            out = out + jax.nn.sigmoid(x @ shared_gate_w.T) * shared
            return out.reshape(b, s, h)
        key = jax.random.key(seed)
        ks = jax.random.split(key, 8)
        scale = 0.02
        return {'hidden_states': jax.random.normal(ks[0], (B, S, H), dtype=jnp.float32), 'router_weight': jax.random.normal(ks[1], (E, H), dtype=jnp.float32) * scale, 'gate_up_proj': jax.random.normal(ks[2], (E, 2 * I_MOE, H), dtype=jnp.float32) * scale, 'down_proj': jax.random.normal(ks[3], (E, H, I_MOE), dtype=jnp.float32) * scale, 'sh_gate_w': jax.random.normal(ks[4], (I_SH, H), dtype=jnp.float32) * scale, 'sh_up_w': jax.random.normal(ks[5], (I_SH, H), dtype=jnp.float32) * scale, 'sh_down_w': jax.random.normal(ks[6], (H, I_SH), dtype=jnp.float32) * scale, 'shared_gate_w': jax.random.normal(ks[7], (1, H), dtype=jnp.float32) * scale}
    _L0_ffn_in = _L0_ffn_setup()
    _d = {'L0_attn_hidden_states': _L0_attn_in['hidden_states'], 'L0_attn_Wq': _L0_attn_in['Wq'], 'L0_attn_Wk': _L0_attn_in['Wk'], 'L0_attn_Wv': _L0_attn_in['Wv'], 'L0_attn_Wo': _L0_attn_in['Wo'], 'L0_attn_bo': _L0_attn_in['bo'], 'L0_ffn_router_weight': _L0_ffn_in['router_weight'], 'L0_ffn_gate_up_proj': _L0_ffn_in['gate_up_proj'], 'L0_ffn_down_proj': _L0_ffn_in['down_proj'], 'L0_ffn_sh_gate_w': _L0_ffn_in['sh_gate_w'], 'L0_ffn_sh_up_w': _L0_ffn_in['sh_up_w'], 'L0_ffn_sh_down_w': _L0_ffn_in['sh_down_w'], 'L0_ffn_shared_gate_w': _L0_ffn_in['shared_gate_w']}
    _x0 = _d['L0_attn_hidden_states']
    _d['L0_attn_hidden_states'] = jax.random.normal(jax.random.fold_in(jax.random.key(seed), 1), (2, 1024, 256), dtype=_x0.dtype)
    del _x0
    return _d

def reference(L0_attn_hidden_states, L0_attn_Wq, L0_attn_Wk, L0_attn_Wv, L0_attn_Wo, L0_attn_bo, L0_ffn_router_weight, L0_ffn_gate_up_proj, L0_ffn_down_proj, L0_ffn_sh_gate_w, L0_ffn_sh_up_w, L0_ffn_sh_down_w, L0_ffn_shared_gate_w):

    def _L0_attn_ref(hidden_states, Wq, Wk, Wv, Wo, bo):
        import jax, jax.numpy as jnp
        import numpy as np
        import math
        N_HEADS = 32
        N_GROUPS = 8
        D_HEAD = 64
        D_MODEL = 256

        def _rope(x):
            S, D = (x.shape[-2], x.shape[-1])
            inv_freq = 1.0 / 10000.0 ** (jnp.arange(0, D, 2, dtype=jnp.float32) / D)
            freqs = jnp.arange(S, dtype=jnp.float32)[:, None] * inv_freq[None, :]
            cos = jnp.repeat(jnp.cos(freqs), 2, axis=-1)
            sin = jnp.repeat(jnp.sin(freqs), 2, axis=-1)
            x2 = x.reshape(*x.shape[:-1], D // 2, 2)
            rot = jnp.stack([-x2[..., 1], x2[..., 0]], axis=-1).reshape(x.shape)
            return x * cos + rot * sin
        N, S, _ = hidden_states.shape
        n_rep = N_HEADS // N_GROUPS
        q = (hidden_states @ Wq).reshape(N, S, N_HEADS, D_HEAD).transpose(0, 2, 1, 3)
        k = (hidden_states @ Wk).reshape(N, S, N_GROUPS, D_HEAD).transpose(0, 2, 1, 3)
        v = (hidden_states @ Wv).reshape(N, S, N_GROUPS, D_HEAD).transpose(0, 2, 1, 3)
        q = _rope(q)
        k = _rope(k)
        k = jnp.repeat(k, n_rep, axis=1)
        v = jnp.repeat(v, n_rep, axis=1)
        scores = jnp.einsum('bhsd,bhtd->bhst', q, k)
        slopes = 2.0 ** (-(jnp.arange(1, N_HEADS + 1, dtype=jnp.float32) * 8.0 / N_HEADS))
        pos = jnp.arange(S, dtype=jnp.float32)
        alibi = -jnp.abs(pos[:, None] - pos[None, :])[None] * slopes[:, None, None]
        scores = (scores + alibi[None]) / math.sqrt(D_HEAD)
        scores = 30.0 * jnp.tanh(scores / 30.0)
        causal = jnp.tril(jnp.ones((S, S), dtype=bool))
        scores = jnp.where(causal[None, None], scores, -jnp.inf)
        probs = jax.nn.softmax(scores, axis=-1)
        ctx = jnp.einsum('bhst,bhtd->bhsd', probs, v)
        ctx = ctx.transpose(0, 2, 1, 3).reshape(N, S, N_HEADS * D_HEAD)
        return ctx @ Wo + bo

    def _L0_ffn_ref(hidden_states, router_weight, gate_up_proj, down_proj, sh_gate_w, sh_up_w, sh_down_w, shared_gate_w):
        import jax, jax.numpy as jnp
        import numpy as np
        E = 8
        TOP_K = 2
        H = 256
        I_MOE = 176
        I_SH = 704
        B, S = (2, 256)

        def _moe_forward(hidden_states, router_weight, gate_up_proj, down_proj, sh_gate_w, sh_up_w, sh_down_w, shared_gate_w):
            b, s, h = hidden_states.shape
            x = hidden_states.reshape(-1, h)
            shared = jnp.einsum('ti,hi->th', jax.nn.silu(x @ sh_gate_w.T) * (x @ sh_up_w.T), sh_down_w)
            logits = x @ router_weight.T
            probs = jax.nn.softmax(logits.astype(jnp.float32), axis=-1)
            top_v, top_i = jax.lax.top_k(probs, TOP_K)
            top_v = top_v / top_v.sum(axis=-1, keepdims=True)
            combine = (jax.nn.one_hot(top_i, E, dtype=top_v.dtype) * top_v[..., None]).sum(axis=1)
            out = jnp.zeros_like(x)
            for e in range(E):
                gu = x @ gate_up_proj[e].T
                gate, up = (gu[:, :I_MOE], gu[:, I_MOE:])
                cur = jax.nn.silu(gate) * up @ down_proj[e].T
                out = out + cur * combine[:, e:e + 1]
            out = out + jax.nn.sigmoid(x @ shared_gate_w.T) * shared
            return out.reshape(b, s, h)
        return _moe_forward(hidden_states, router_weight, gate_up_proj, down_proj, sh_gate_w, sh_up_w, sh_down_w, shared_gate_w)
    x = L0_attn_hidden_states
    x = x + _layernorm(_L0_attn_ref(_layernorm(x, axis=-1), L0_attn_Wq, L0_attn_Wk, L0_attn_Wv, L0_attn_Wo, L0_attn_bo), axis=-1)
    x = x + _layernorm(_L0_ffn_ref(_layernorm(x, axis=-1), L0_ffn_router_weight, L0_ffn_gate_up_proj, L0_ffn_down_proj, L0_ffn_sh_gate_w, L0_ffn_sh_up_w, L0_ffn_sh_down_w, L0_ffn_shared_gate_w), axis=-1)
    return x

_drawn_inputs = setup_inputs


def setup_inputs(seed=0):
    import zlib

    import numpy as np

    out = dict(_drawn_inputs(seed))
    spreads = {'L0_attn_bo': (0.0, 0.1)}
    factors = {}
    for name, (base, spread) in spreads.items():
        noise = np.random.default_rng([zlib.crc32(name.encode()), seed]).standard_normal(out[name].shape)
        drawn = base * np.exp(spread * noise) if base else spread * noise
        out[name] = jnp.asarray(drawn.astype(out[name].dtype))
    for name, factor in factors.items():
        out[name] = (out[name] * factor).astype(out[name].dtype)
    return out
```

```python
from contextlib import ExitStack

import numpy as np
import concourse.bass as bass
from concourse import mybir

F32 = mybir.dt.float32
F32R = mybir.dt.float32r
U32 = mybir.dt.uint32
ALU = mybir.AluOpType
ACT = mybir.ActivationFunctionType

P = 128
B, S, D = 2, 1024, 256
TOK = B * S
NB = TOK // P
H, G, DH = 32, 8, 64
R = H // G
KT = D // P
CH = 512
NE, IM, ISH = 8, 176, 704
HID = NE * IM + ISH
NT = -(-HID // P)
NG = NE + 1
NR = NG + 1
EPS = 1e-5
CAP = 30.0
VW = DH + 2
TPC = CH // P



def unit_pieces(u):
    def diagonal(hh, c):
        return [(hh, 4 * c, CH * c, CH, 0), (hh, 4 * c + 3, CH * c + 384, 128, CH),
                (hh, 4 * c + 1, CH * c + 128, 384, CH + 128)]

    def rest(c):
        return [(hh, 4 * c + 2, CH * c + 256, 256, 256 * hh) for hh in range(2)]

    def full(hh, t):
        return [(hh, t, CH, CH, 0), (hh, t + 1, CH, CH, CH)]

    return [diagonal(0, 0), diagonal(1, 0), rest(0), full(0, 0), full(0, 2), diagonal(0, 1),
            full(1, 0), full(1, 2), diagonal(1, 1), rest(1)][u]


PU = 10
NU = 2 * PU
WIDTH = [sum(p[3] for p in unit_pieces(u)) for u in range(PU)]
MASKED = [u for u in range(PU) if u not in (3, 4, 6, 7)]
NM = 2 * len(MASKED)
CHUNK_END = {2: 0, 9: 1}
CHUNK_START = {0: 0, 3: 1}


def masked_count(n, u):
    p, v = divmod(u, PU)
    return NM * n + len(MASKED) * p + MASKED.index(v) + 1


def wait_apart(eng, sem, value, passed):
    eng.wait_ge(sem, value)
    if not isinstance(value, int):
        eng.sem_inc(passed, 1)


class Steps:

    def __init__(self, eng, sem):
        self.eng, self.sem, self.base, self.k = eng, sem, 0, 0

    def add(self, instruction):
        instruction.then_inc(self.sem, 1)
        self.k += 1
        return self.k

    def wait(self, k=None):
        self.eng.wait_ge(self.sem, self.base + (self.k if k is None else k))

    def wait_apart(self, passed):
        wait_apart(self.eng, self.sem, self.base + self.k, passed)


def build(nc, x, wq, wk, wv, wo, bo, wf, wr, cs, al, ident, sel, out):
    with ExitStack() as ctx:
        def sem(name):
            return ctx.enter_context(nc.semaphore(name))

        def sb(stack, name, shape, dt=F32):
            return stack.enter_context(nc.sbuf_tensor(name, shape, dt))

        ks_dram = nc.dram_tensor("ks_scratch", (4, G * 32, TOK), F32, kind="Internal").ap()
        ka_dram = nc.dram_tensor("ka_scratch", (G * 4, S), F32, kind="Internal").ap()

        PS = ctx.enter_context(nc.psum_tensor("PS", [P, 8, CH], F32))
        SC = PS[:, 0:4, :].rearrange("p (b k) n -> p b (k n)", b=2)
        PV = PS[:, 4:6, :]
        SD = PS[:, 6:8, :]

        XTh = sb(ctx, "XTh", [P, KT, TOK], F32R)
        XTl = sb(ctx, "XTl", [P, KT, TOK], F32R)
        yacc = sb(ctx, "yacc", [P, NB, D])
        idn = sb(ctx, "idn", [P, P])
        stats = sb(ctx, "stats", [P, NB, 6])
        mv = sb(ctx, "mv", [P, NB, 2])
        vareps = sb(ctx, "vareps", [P, NB])
        std = sb(ctx, "std", [P, NB])
        rstd = sb(ctx, "rstd", [P, NB])
        newton = sb(ctx, "newton", [P, NB])

        att = ExitStack()
        KKa = [sb(att, f"KKa{b}", [P, S], F32R) for b in range(B)]
        KKb = [sb(att, f"KKb{b}", [P, S], F32R) for b in range(B)]
        ST = sb(att, "ST", [P, 4, S], F32R)
        tc = sb(att, "tc", [P, 2, CH])
        ts = sb(att, "ts", [P, 2, CH])
        EO = sb(att, "EO", [P, 2, CH])
        CS = sb(att, "CS", [P, 2, S])
        V = sb(att, "V", [P, NB, G, VW])
        WQr = sb(att, "WQr", [P, KT, 2, P])
        WQh = sb(att, "WQh", [P, KT, 2, P], F32R)
        WQl = sb(att, "WQl", [P, KT, 2, P], F32R)
        WOr = sb(att, "WOr", [P, 2, D])
        WOh = sb(att, "WOh", [P, 2, D], F32R)
        WOl = sb(att, "WOl", [P, 2, D], F32R)
        CTX = sb(att, "CTX", [P, TPC, 2, DH])
        RC = sb(att, "RC", [P, 2, TPC])
        CTh = sb(att, "CTh", [P, TPC, P], F32R)
        CTl = sb(att, "CTl", [P, TPC, P], F32R)
        pro = ExitStack()
        X = sb(pro, "X", [P, NB, D])
        Wr = sb(pro, "Wr", [P, 2, KT, CH])
        Wh = sb(pro, "Wh", [P, 2, KT, CH], F32R)
        Wl = sb(pro, "Wl", [P, 2, KT, CH], F32R)
        ALr = sb(pro, "ALr", [48, S])
        pro.close()
        QSa = sb(att, "QSa", [P, R, S], F32R)
        QSb = sb(att, "QSb", [P, R, S], F32R)
        PR = sb(att, "PR", [P, 4, 2 * CH])
        ALh = sb(att, "ALh", [48, S], F32R)
        att.close()

        ffn = ExitStack()
        X2 = sb(ffn, "X2", [P, NB, D])
        CT = sb(ffn, "CT", [P, TOK], F32R)
        SL = sb(ffn, "SL", [P, NT * P], F32R)
        WFr = sb(ffn, "WFr", [P, 2, 3 * D])
        WFh = sb(ffn, "WFh", [P, NT, 3 * D], F32R)
        router = ExitStack()
        SLr = sb(router, "SLr", [P, NT * P])
        router.close()
        WFl = sb(ffn, "WFl", [P, NT, 3 * D], F32R)
        router = ExitStack()
        Rr = sb(router, "Rr", [P, KT, NR])
        Rh = sb(router, "Rh", [P, KT, NR], F32R)
        Rl = sb(router, "Rl", [P, KT, NR], F32R)
        LG = sb(router, "LG", [P, NB, NR])
        top = sb(router, "top", [P, NB, 8])
        topi = sb(router, "topi", [P, NB, 8], U32)
        topf = sb(router, "topf", [P, NB, 8])
        ex = sb(router, "ex", [P, 2, NB])
        den = sb(router, "den", [P, 2, NB])
        wt = sb(router, "wt", [P, 3, NB])
        CB = sb(router, "CB", [P, NB, NG])
        CB2 = sb(router, "CB2", [P, NB, NG])
        CBh = sb(router, "CBh", [P, NB, NG], F32R)
        CBx = sb(router, "CBx", [P, NB, 2 * NG])
        router.close()
        Hh = sb(ffn, "Hh", [P, 2, CH], F32R)
        Hl = sb(ffn, "Hl", [P, 2, CH], F32R)
        ffn.close()
        sg, hd, Y, O = (yacc[:, 4 * i:4 * i + 4, :].rearrange("p (a b) d -> p a (b d)", a=2) for i in range(4))
        Y, O = (t.rearrange("p a (b d) -> p (a b) d", b=2) for t in (Y, O))

        NX = NB // TPC
        x_in = [sem(f"x_in{i}") for i in range(NX)]
        kv_in, cs_in, id_in, al_in, bo_in, q_in, o_in = (sem(n) for n in
            ("kv_in", "cs_in", "id_in", "al_in", "bo_in", "q_in", "o_in"))
        dve_step, pool_step = sem("dve_step"), sem("pool_step")
        dve_passed, pool_passed = sem("dve_passed"), sem("pool_passed")
        var_ready, std_ready, xn_ready = sem("var_ready"), sem("std_ready"), sem("xn_ready")
        xt_psum, xt_high, xt_low = sem("xt_psum"), sem("xt_high"), sem("xt_low")
        kvw_ready = sem("kvw_ready")
        v_psum, v_ready, v_ones = sem("v_psum"), sem("v_ready"), sem("v_ones")
        al_ready, ka_stored, slope_rows = sem("al_ready"), sem("ka_stored"), sem("slope_rows")
        k_stored = [sem(f"k_stored{i}") for i in range(2)]
        kk_in = [sem(f"kk_in{b}") for b in range(B)]
        qs_in = [sem(f"qs_in{p}") for p in range(2)]
        proj_done, proj_read, rope_done = sem("proj_done"), sem("proj_read"), sem("rope_done")
        wq_ready, wo_ready = sem("wq_ready"), sem("wo_ready")
        qk_done, tanh_done, exp_done, mask_done, pv_done = (sem(n) for n in
            ("qk_done", "tanh_done", "exp_done", "mask_done", "pv_done"))
        norm_done, ctxT_done, split_done, y_done, y_added = (sem(n) for n in
            ("norm_done", "ctxT_done", "split_done", "y_done", "y_added"))
        x2_in = sem("x2_in")
        r_in, rw_ready, lg_done, lg_read, cb_ready, cbT_done, cbT_read, ct_zero = (sem(n) for n in
            ("r_in", "rw_ready", "lg_done", "lg_read", "cb_ready", "cbT_done", "cbT_read", "ct_zero"))
        gap_ready, e2_ready, sel_zero, sel_in, sel_ready = (sem(n) for n in
            ("gap_ready", "e2_ready", "sel_zero", "sel_in", "sel_ready"))
        wf_in = [sem(f"wf_in{i}") for i in range(2)]
        wfh_ready, wfl_ready = sem("wfh_ready"), sem("wfl_ready")
        guc_done, silu_done, hid_done, hh_done, hl_done, down_done = (sem(n) for n in
            ("guc_done", "silu_done", "hid_done", "hh_done", "hl_done", "down_done"))
        fy_done, fy_read, o_ready, o_out = (sem(n) for n in ("fy_done", "fy_read", "o_ready", "o_out"))

        NPROJ = 8
        QT = 16 * 12
        KL = 16 * 7

        block = ctx.enter_context(nc.Block())

        @block.sync
        def _(sp):
            xv = x.rearrange("(q t p) d -> q p t d", p=P, t=TPC)
            for i in range(NX):
                sp.dma_start(X[:, TPC * i:TPC * (i + 1), :], xv[i]).then_inc(x_in[i], 16)
                if i == 0:
                    sp.dma_start(idn[:], ident).then_inc(id_in, 16)
            sp.dma_start(Wr[:, 1], wv).then_inc(kv_in, 16)
            sp.dma_start(Wr[:, 0], wk).then_inc(kv_in, 16)
            sp.dma_start(CS[:], cs).then_inc(cs_in, 16)
            sp.dma_start(WQr[:], wq[0]).then_inc(q_in, 16)
            sp.dma_start(WOr[:], wo[0]).then_inc(o_in, 16)
            sp.dma_start(ALr[:], al).then_inc(al_in, 16)
            sp.dma_start(yacc[:], bo.partition_broadcast(P).unsqueeze(1).broadcast_to([P, NB, D])
                         ).then_inc(bo_in, 16)
            for i in range(NPROJ):
                s, q = divmod(i, 4)
                sp.wait_ge(rope_done, i + 1)
                sp.dma_start(ks_dram[:, P * s:P * (s + 1), CH * q:CH * (q + 1)].rearrange("k p n -> p k n"),
                             ST[:, :, CH * (i % 2):CH * (i % 2 + 1)].bitcast(F32)).then_inc(k_stored[i % 2], 16)
            sp.wait_ge(al_ready, 1)
            sp.dma_start(ka_dram, ALh[0:32, :].bitcast(F32)).then_inc(ka_stored, 16)
            for h in range(R):
                sp.dma_start(QSb[64:68, h, :].bitcast(F32), ALh[32 + 4 * h:36 + 4 * h, :].bitcast(F32)).then_inc(slope_rows, 16)
            for i in range(2):
                sp.wait_ge(k_stored[i], 16 * NPROJ // 2)
            sp.wait_ge(ka_stored, 16)

            def load_keys(g, b):
                for quarter in range(4):
                    sp.dma_start(KKa[b][32 * quarter:32 * quarter + 32, :].bitcast(F32),
                                 ks_dram[quarter % 2, bass.ds(32 * g, 32), S * b:S * (b + 1)]).then_inc(kk_in[b], 16)
                for quarter in range(2):
                    sp.dma_start(KKb[b][32 * quarter:32 * quarter + 32, :].bitcast(F32),
                                 ks_dram[2 + quarter, bass.ds(32 * g, 32), S * b:S * (b + 1)]).then_inc(kk_in[b], 16)
                sp.dma_start(KKb[b][64:68, :].bitcast(F32), ka_dram[bass.ds(4 * g, 4), :]).then_inc(kk_in[b], 16)

            def move_queries(p):
                for h in (2 * p, 2 * p + 1):
                    for kind in range(4):
                        sp.dma_start(QSa[32 * kind:32 * kind + 32, h, :].bitcast(F32),
                                     ST[32 * h:32 * h + 32, kind, :].bitcast(F32)).then_inc(qs_in[p], 16)
                    for kind in range(2):
                        sp.dma_start(QSb[32 * kind:32 * kind + 32, h, :].bitcast(F32),
                                     ST[32 * h:32 * h + 32, kind, :].bitcast(F32)).then_inc(qs_in[p], 16)

            load_keys(0, 0)
            sp.wait_ge(rope_done, NPROJ + 2)
            move_queries(0)
            move_queries(1)
            load_keys(0, 1)

            def body(g, last=False):
                for b in range(B):
                    n = 2 * g + b
                    if not last:
                        if b == 0:
                            sp.wait_ge(wq_ready, g + 1)
                            sp.dma_start(WQr[:], wq[bass.ds(g + 1, 1)].squeeze(0)).then_inc(q_in, 16)
                        else:
                            sp.wait_ge(wo_ready, g + 1)
                            sp.dma_start(WOr[:], wo[bass.ds(g + 1, 1)].squeeze(0)).then_inc(o_in, 16)
                    if not (last and b == B - 1):
                        sp.wait_ge(rope_done, NPROJ + 2 * n + 4)
                        sp.wait_ge(qk_done, NU * n + PU)
                        move_queries(0)
                        sp.wait_ge(qk_done, NU * n + NU)
                        move_queries(1)
                        if not last:
                            load_keys(g + 1, b)

            body(0)
            with sp.Fori(1, G - 1) as g:
                body(g)
            body(G - 1, last=True)

            sp.wait_ge(y_added, 2 * 4 * B * G)
            sp.dma_start(X2[:], x.rearrange("(t p) d -> p t d", p=P)).then_inc(x2_in, 16)
            sp.dma_start(Rr[:], wr).then_inc(r_in, 16)
            sp.wait_ge(sel_zero, 1)
            sp.dma_start(SLr[0:2 * NG, :], sel).then_inc(sel_in, 16)
            for j in range(NT):
                if j >= 2:
                    sp.wait_ge(wfl_ready, j - 1)
                sp.dma_start(WFr[:, j % 2], wf[j]).then_inc(wf_in[j % 2], 16)
            ov = out.rearrange("(q t p) d -> q p t d", p=P, t=TPC)
            with sp.Fori(0, NX) as q:
                sp.wait_ge(o_ready, q + 1)
                sp.dma_start(ov[bass.ds(q, 1)].squeeze(0), O[:]).then_inc(o_out, 16)
            sp.wait_ge(o_out, 16 * NX)

        @block.tensor
        def _(pe):
            def three(dst, ah, al_, bh, bl, kts, first=True, last=True, **kw):
                terms = [(a(k), b(k)) for k in kts for a, b in ((ah, bh), (ah, bl), (al_, bh))]
                for i, (a, b) in enumerate(terms):
                    mm = pe.matmul(dst, a, b, start=first and i == 0, stop=last and i == len(terms) - 1, **kw)
                return mm

            pe.wait_ge(id_in, 16)
            for i in range(NB // 2):
                pe.wait_ge(xn_ready, 2 * i + 2)
                if i >= 2:
                    pe.wait_ge(xt_high, i - 1)
                    pe.wait_ge(xt_low, i - 1)
                dst = PS[:, i % 2, :].rearrange("p (k t) -> p k t", k=KT)
                for t in range(2):
                    for k in range(KT):
                        mm = pe.transpose(dst[:, k, P * t:P * (t + 1)], X[:, 2 * i + t, P * k:P * (k + 1)], idn[:])
                mm.then_inc(xt_psum, 1)
            pe.wait_ge(xt_high, NB // 2)
            pe.wait_ge(xt_low, NB // 2)
            pe.wait_ge(kvw_ready, 3)
            def project(w_hi, w_lo, tokens, i):
                if not isinstance(i, int) or i >= 1:
                    pe.wait_ge(proj_read, i)
                for eo in range(2):
                    mm = three(SD[:, eo, :], lambda k: w_hi(k, eo), lambda k: w_lo(k, eo),
                               lambda k: XTh[:, k, tokens], lambda k: XTl[:, k, tokens], range(KT))
                mm.then_inc(proj_done, 1)

            def values(t):
                if t >= 4:
                    pe.wait_ge(v_ready, t - 3)
                tok = slice(P * t, P * (t + 1))
                three(PS[:, 2 + t % 4, :], lambda k: XTh[:, k, tok], lambda k: XTl[:, k, tok],
                      lambda k: Wh[:, 1, k, :], lambda k: Wl[:, 1, k, :], range(KT)).then_inc(v_psum, 1)

            for i in range(NPROJ):
                s, q = divmod(i, 4)
                project(lambda k, eo: Wh[:, 0, k, 256 * s + P * eo:256 * s + P * (eo + 1)],
                        lambda k, eo: Wl[:, 0, k, 256 * s + P * eo:256 * s + P * (eo + 1)],
                        slice(CH * q, CH * (q + 1)), i)
                values(2 * i)
                values(2 * i + 1)

            def queries(n, b, c):
                project(lambda k, eo: WQh[:, k, eo, :], lambda k, eo: WQl[:, k, eo, :],
                        slice(S * b + CH * c, S * b + CH * (c + 1)), NPROJ + 2 * n + c)

            pe.wait_ge(wq_ready, 1)
            queries(0, 0, 0)
            queries(0, 0, 1)
            pe.wait_ge(v_ready, NB)
            pe.wait_ge(v_ones, 1)
            pe.wait_ge(slope_rows, 16 * R)

            def scores(n, g, b, u):
                p, v = divmod(u, PU)
                if u == 0:
                    pe.wait_ge(kk_in[b], KL * (g + 1))
                if v == 0:
                    pe.wait_ge(qs_in[p], QT * (n + 1))
                U = NU * n + u
                if not isinstance(U, int) or U >= 2:
                    pe.wait_ge(tanh_done, U - 1)
                for hh, t, s0, w, col in unit_pieces(v):
                    dst = SC[:, u % 2, col:col + w]
                    keys, q = slice(P * t, P * (t + 1)), slice(s0, s0 + w)
                    pe.matmul(dst, KKa[b][:, keys], QSa[:, 2 * p + hh, q], start=True, stop=False)
                    mm = pe.matmul(dst, KKb[b][0:68, keys], QSb[0:68, 2 * p + hh, q], start=False, stop=True)
                mm.then_inc(qk_done, 1)

            def context(n, g, b, u):
                p, v = divmod(u, PU)
                if v in MASKED:
                    pe.wait_ge(mask_done, masked_count(n, u))
                else:
                    pe.wait_ge(exp_done, NU * n + u + 1)
                if v in CHUNK_START:
                    m = 4 * n + 2 * p + CHUNK_START[v]
                    if not isinstance(m, int) or m >= 1:
                        pe.wait_ge(norm_done, m)
                started = {0: v not in (0, 3), 1: v not in (1, 6)}
                pieces = unit_pieces(v)
                for i, (hh, t, s0, w, col) in enumerate(pieces):
                    for k in range(w // P):
                        blk = (s0 // P + k) % TPC
                        mm = pe.matmul(PV[:, hh, VW * blk:VW * blk + DH + 1],
                                       PR[:, u % 4, col + P * k:col + P * (k + 1)],
                                       V[:, NB // B * b + t, :, :].rearrange("p g w -> p (g w)")[:, bass.ds(VW * g, DH + 1)],
                                       start=not started[hh], stop=v in CHUNK_END and k == w // P - 1,
                                       skip_group_check=True)
                        started[hh] = True
                mm.then_inc(pv_done, 1)

            def turn(m, projections):
                pe.wait_ge(norm_done, m + 1)
                pe.wait_ge(proj_read, projections)
                if not isinstance(m, int) or m >= 1:
                    pe.wait_ge(split_done, m)
                for k in range(TPC):
                    mm = pe.transpose(SD[:, 0, P * k:P * (k + 1)], CTX[:, k, :, :].rearrange("p h d -> p (h d)"), idn[:])
                mm.then_inc(ctxT_done, 1)

            def project_out(m, p, half):
                if half == 0:
                    pe.wait_ge(split_done, m + 1)
                if not isinstance(m, int) or 2 * m + half >= 1:
                    pe.wait_ge(y_added, 2 * m + half)
                for i in range(2):
                    k = 2 * half + i
                    mm = three(SD[:, 1, D * i:D * (i + 1)], lambda _: CTh[:, k, :], lambda _: CTl[:, k, :],
                               lambda _: WOh[:, p, :], lambda _: WOl[:, p, :], [0])
                mm.then_inc(y_done, 1)

            def side(n, g, b, u, first, last):
                p, v = divmod(u, PU)
                m = 4 * n + 2 * p
                before = not (first and b == 0 and p == 0)
                more = not (last and b == B - 1)
                projections = NPROJ + 2 * n + 2 + (2 * p if more else 0)
                if v == 0 and p == 1 and more:
                    pe.wait_ge(split_done, m - 1)
                    pe.wait_ge(y_added, 2 * m - 2)
                    queries(n + 1, (b + 1) % B, 1)
                if v == 2 and before:
                    turn(m - 1, projections)
                if v in (3, 4) and before:
                    project_out(m - 1, 1 - p, v - 3)
                if v == 5:
                    turn(m, projections)
                if v in (6, 7):
                    if v == 6 and b == 0 and p == 0:
                        pe.wait_ge(wo_ready, g + 1)
                    project_out(m, p, v - 6)
                if v == 8 and p == 0 and more:
                    if b == B - 1:
                        pe.wait_ge(wq_ready, g + 2)
                    pe.wait_ge(split_done, m + 1)
                    pe.wait_ge(y_added, 2 * m + 2)
                    queries(n + 1, (b + 1) % B, 0)

            def body(g, first=False, last=False):
                for b in range(B):
                    n = 2 * g + b
                    for u in range(NU):
                        if u + 2 < NU:
                            scores(n, g, b, u + 2)
                        elif b == 0:
                            scores(n + 1, g, 1, u + 2 - NU)
                        elif not last:
                            scores(n + 1, g + 1, 0, u + 2 - NU)
                        context(n, g, b, u)
                        side(n, g, b, u, first, last)

            scores(0, 0, 0, 0)
            scores(0, 0, 0, 1)
            body(0, first=True)
            with pe.Fori(1, G - 1) as g:
                body(g)
            body(G - 1, last=True)
            M = 4 * B * G
            turn(M - 1, NPROJ + 2 * B * G)
            project_out(M - 1, 1, 0)
            project_out(M - 1, 1, 1)

            for i in range(NB // 2):
                pe.wait_ge(xn_ready, NB + 2 * i + 2)
                if i >= 2:
                    pe.wait_ge(xt_high, NB // 2 + i - 1)
                    pe.wait_ge(xt_low, NB // 2 + i - 1)
                dst = PS[:, i % 2, :].rearrange("p (k t) -> p k t", k=KT)
                for t in range(2):
                    for k in range(KT):
                        mm = pe.transpose(dst[:, k, P * t:P * (t + 1)], yacc[:, 2 * i + t, P * k:P * (k + 1)], idn[:])
                mm.then_inc(xt_psum, 1)
            pe.wait_ge(xt_high, NB)
            pe.wait_ge(xt_low, NB)
            pe.wait_ge(rw_ready, 2)
            for t in range(NB):
                tok = slice(P * t, P * (t + 1))
                mm = three(PS[:, 2, 16 * t:16 * t + NR], lambda k: XTh[:, k, tok], lambda k: XTl[:, k, tok],
                           lambda k: Rh[:, k, :], lambda k: Rl[:, k, :], range(KT))
            mm.then_inc(lg_done, 1)

            def gate_up(q, j):
                if not isinstance(q, int) or q >= 1:
                    pe.wait_ge(hid_done, NT * q + j - (j > 0))
                elif j >= 2:
                    pe.wait_ge(hid_done, j - 1)
                tok = bass.ds(CH * q, CH)
                for part in range(2):
                    three(PS[:, 3 * (j % 2) + part, :], lambda k: WFh[:, j, 256 * part + P * k:256 * part + P * (k + 1)],
                          lambda k: WFl[:, j, 256 * part + P * k:256 * part + P * (k + 1)],
                          lambda k: XTh[:, k, tok], lambda k: XTl[:, k, tok], range(KT))
                pe.matmul(PS[:, 3 * (j % 2) + 2, :], SL[:, P * j:P * (j + 1)], CT[:, tok], start=True, stop=True
                          ).then_inc(guc_done, 1)

            def down(q, j):
                pe.wait_ge(hh_done, NT * q + j + 1)
                pe.wait_ge(hl_done, NT * q + j + 1)
                if j == 0 and (not isinstance(q, int) or q >= 1):
                    pe.wait_ge(fy_read, q)
                for t in range(TPC):
                    tok = slice(P * t, P * (t + 1))
                    w = slice(512, 512 + D)
                    dst = PS[:, 6 + t // 2, D * (t % 2):D * (t % 2 + 1)]
                    for i, (a, w_) in enumerate(((Hh, WFh), (Hh, WFl), (Hl, WFh))):
                        mm = pe.matmul(dst, a[:, j % 2, tok], w_[:, j, w], start=j == 0 and i == 0 and t % 2 == 0,
                                       stop=j == NT - 1 and i == 2, skip_group_check=True)
                mm.then_inc(down_done, 1)

            def chunk(q, first=False):
                for j in range(NT + 1):
                    if j < NT:
                        if first:
                            pe.wait_ge(wfh_ready, j + 1)
                            pe.wait_ge(wfl_ready, j + 1)
                        gate_up(q, j)
                    if j >= 1:
                        down(q, j - 1)

            for i in range(NB // 4):
                pe.wait_ge(cb_ready, 2)
                if i >= 1:
                    pe.wait_ge(cbT_read, i)
                for t in range(4):
                    mm = pe.transpose(PS[0:2 * NG, 3, P * t:P * (t + 1)], CBx[:, 4 * i + t, :], idn[:])
                mm.then_inc(cbT_done, 1)
            pe.wait_ge(cbT_read, NB // 4)
            pe.wait_ge(sel_ready, 1)
            pe.wait_ge(ct_zero, 1)
            chunk(0, first=True)
            with pe.Fori(1, NX) as q:
                chunk(q)

        @block.scalar
        def _(act):
            def roots(i):
                act.wait_ge(var_ready, i + 1)
                act.activation(std[:, TPC * (i % NX):TPC * (i % NX + 1)], vareps[:, TPC * (i % NX):TPC * (i % NX + 1)],
                               ACT.Sqrt).then_inc(std_ready, 1)

            def expert_weights(j):
                act.wait_ge(wf_in[j % 2], 16 * (j // 2 + 1))
                act.copy(WFh[:, j, :], WFr[:, j % 2, :]).then_inc(wfh_ready, 1)

            def transposed(i, total):
                act.wait_ge(xt_psum, total + i + 1)
                act.copy(XTh[:, :, 2 * P * i:2 * P * (i + 1)], PS[:, i % 2, :].rearrange("p (k t) -> p k t", k=KT)
                         ).then_inc(xt_high, 1)

            for i in range(NX):
                roots(i)
                if i == 0:
                    act.wait_ge(kv_in, 32)
                    act.copy(Wh[:], Wr[:]).then_inc(kvw_ready, 1)
                if i >= 1:
                    transposed(2 * i - 2, 0)
                    transposed(2 * i - 1, 0)
            transposed(2 * NX - 2, 0)
            transposed(2 * NX - 1, 0)
            for t in range(NB):
                act.wait_ge(v_psum, t + 1)
                act.copy(V[:, t, :, 0:DH], PS[:, 2 + t % 4, :].rearrange("p (g d) -> p g d", g=G)).then_inc(v_ready, 1)
            act.wait_ge(al_in, 16)
            act.wait_ge(proj_done, NPROJ + 1)
            act.copy(ALh[:], ALr[:]).then_inc(al_ready, 1)

            def capped(n, u):
                U = NU * n + u
                act.wait_ge(qk_done, U + 1)
                if not isinstance(U, int) or U >= 4:
                    act.wait_ge(pv_done, U - 3)
                w = WIDTH[u % PU]
                act.activation(PR[:, u % 4, 0:w], SC[:, u % 2, 0:w], ACT.Tanh, scale=1.0 / (CAP * DH ** 0.5)
                               ).then_inc(tanh_done, 1)

            def exponential(n, u):
                act.wait_ge(tanh_done, NU * n + u + 1)
                w = WIDTH[u % PU]
                act.activation(PR[:, u % 4, 0:w], PR[:, u % 4, 0:w], ACT.Exp, scale=CAP).then_inc(exp_done, 1)

            def body(g, last=False):
                for b in range(B):
                    n = 2 * g + b
                    for u in range(NU):
                        if u + 1 < NU:
                            capped(n, u + 1)
                        elif not (last and b == B - 1):
                            capped(n + 1, 0)
                        exponential(n, u)

            capped(0, 0)
            body(0)
            with act.Fori(1, G - 1) as g:
                body(g)
            body(G - 1, last=True)

            for i in range(2 * NX):
                roots(NX + i)
                if i == 0:
                    act.wait_ge(r_in, 16)
                    act.copy(Rh[:], Rr[:]).then_inc(rw_ready, 1)
                    act.wait_ge(sel_in, 16)
                    act.copy(SL[:], SLr[:]).then_inc(sel_ready, 1)
                    expert_weights(0)
                    expert_weights(1)
                if i > NX:
                    transposed(2 * (i - NX) - 2, NB // 2)
                    transposed(2 * (i - NX) - 1, NB // 2)
            transposed(2 * NX - 2, NB // 2)
            transposed(2 * NX - 1, NB // 2)
            act.wait_ge(gap_ready, 2)
            act.activation(ex[:], ex[:], ACT.Exp).then_inc(e2_ready, 1)

            def chunk(q, first=False):
                for j in range(NT):
                    if first and j + 2 < NT:
                        expert_weights(j + 2)
                    n = NT * q + j
                    act.wait_ge(guc_done, n + 1)
                    if not first or j >= 2:
                        act.wait_ge(hid_done, n - (j > 0))
                    act.activation(sg[:, j % 2, :], PS[:, 3 * (j % 2), :], ACT.Silu).then_inc(silu_done, 1)
                    if j >= 1:
                        high(q, j - 1, first)
                high(q, NT - 1, first)
                act.wait_ge(down_done, NT * q + NT)
                if not first:
                    act.wait_ge(o_ready, q)
                act.copy(Y, PS[:, 6:8, :].rearrange("p b (t d) -> p (b t) d", t=2)).then_inc(fy_read, 1)
                act.wait_ge(var_ready, 3 * NX + q + 1)
                act.activation(std[:, 0:TPC], vareps[:, 0:TPC], ACT.Sqrt).then_inc(std_ready, 1)

            def high(q, j, first):
                n = NT * q + j
                act.wait_ge(hid_done, n + 1)
                if not first or j >= 2:
                    act.wait_ge(down_done, n - (j > 0))
                    act.wait_ge(hl_done, n - (j > 0))
                act.copy(Hh[:, j % 2, :], hd[:, j % 2, :]).then_inc(hh_done, 1)

            chunk(0, first=True)
            with act.Fori(1, NX) as q:
                chunk(q)

        @block.gpsimd
        def _(pool):
            own = Steps(pool, pool_step)
            pool.memset(V[:, :, :, DH:VW], 1.0).then_inc(v_ones, 1)

            def split(raw, hi, lo, ready):
                own.add(pool.tensor_copy(hi[:], raw[:]))
                own.wait()
                pool.tensor_tensor(lo[:], raw[:], hi[:].bitcast(F32), ALU.subtract).then_inc(ready, 1)

            pool.wait_ge(q_in, 16)
            split(WQr, WQh, WQl, wq_ready)

            def body(g, last=False):
                for b in range(B):
                    n = 2 * g + b
                    for u in range(NU):
                        p, v = divmod(u, PU)
                        if v not in MASKED:
                            continue
                        wait_apart(pool, exp_done, NU * n + u + 1, pool_passed)
                        if v in CHUNK_END:
                            spots = [PR[:, u % 4, 0:CH].rearrange("p (a s) -> p a s", a=2)[:, :, 0:P]]
                        else:
                            spots = [PR[:, u % 4, 0:P].unsqueeze(1),
                                     PR[:, u % 4, CH:CH + 2 * P].rearrange("p (a s) -> p a s", a=2)]
                        for spot in spots:
                            done = pool.affine_select(out=spot, in_=spot, compare_op=ALU.is_ge, fill=0.0, base=0,
                                                      pattern=[[0, spot.shape[1]], [1, P]], channel_multiplier=-1)
                        done.then_inc(mask_done, 1)
                        if u == 5 and b == 0:
                            if not isinstance(g, int) or g >= 1:
                                wait_apart(pool, y_done, 16 * g, pool_passed)
                            wait_apart(pool, o_in, 16 * (g + 1), pool_passed)
                            split(WOr, WOh, WOl, wo_ready)
                        if u == 2 and b == 1 and not last:
                            wait_apart(pool, q_in, 16 * (g + 2), pool_passed)
                            wait_apart(pool, proj_done, NPROJ + 4 * g + 4, pool_passed)
                            split(WQr, WQh, WQl, wq_ready)

            body(0)
            per = own.k - 1
            with pool.Fori(1, G - 1) as g:
                own.base, own.k = 1 + per * g, 0
                body(g)
            own.base, own.k = 1 + per * (G - 1), 0
            body(G - 1, last=True)
            pool.wait_ge(y_done, 2 * 4 * B * G)
            pool.wait_ge(y_added, 2 * 4 * B * G)
            pool.memset(SLr[:], 0.0).then_inc(sel_zero, 1)
            pool.memset(CT[:].bitcast(F32), 0.0).then_inc(ct_zero, 1)
            pool.wait_ge(sel_ready, 1)
            for j in range(NT):
                pool.wait_ge(wfh_ready, j + 1)
                pool.tensor_tensor(WFl[:, j, :], WFr[:, j % 2, :], WFh[:, j, :].bitcast(F32), ALU.subtract
                                   ).then_inc(wfl_ready, 1)

        @block.vector
        def _(dve):
            own = Steps(dve, dve_step)

            def layernorm(i, src, dst, signal=None):
                slot = 0 if not isinstance(i, int) else i % NX
                c = slice(TPC * slot, TPC * (slot + 1))
                for t in range(TPC):
                    own.add(dve.bn_stats(stats[:, TPC * slot + t, :], src(t)))
                own.wait_apart(dve_passed)
                for t in range(TPC):
                    own.add(dve.bn_aggr(mv[:, TPC * slot + t, :], stats[:, TPC * slot + t, :]))
                own.wait()
                own.add(dve.tensor_scalar(vareps[:, c], mv[:, c, 1], EPS, None, ALU.add))
                own.wait()
                dve.tensor_copy(newton[:, c], vareps[:, c]).then_inc(var_ready, 1)
                dve.wait_ge(std_ready, i + 1)
                dve.wait_ge(var_ready, i + 1)
                own.add(dve.reciprocal(rstd[:, c], std[:, c]))
                own.wait()
                own.add(dve.tensor_tensor(newton[:, c], rstd[:, c], rstd[:, c], ALU.mult))
                own.wait()
                own.add(dve.tensor_tensor(newton[:, c], newton[:, c], vareps[:, c], ALU.mult))
                own.wait()
                own.add(dve.tensor_scalar(newton[:, c], newton[:, c], -0.5, 1.5, ALU.mult, ALU.add))
                own.wait()
                own.add(dve.tensor_tensor(rstd[:, c], rstd[:, c], newton[:, c], ALU.mult))
                own.wait()
                for t in range(TPC):
                    b = TPC * slot + t
                    done = dve.tensor_scalar(dst(t), src(t), mv[:, b, 0:1], rstd[:, b:b + 1], ALU.subtract, ALU.mult)
                    if signal is None:
                        own.add(done)
                    else:
                        done.then_inc(signal, 1)

            def transposed(i, total):
                dve.wait_ge(xt_high, total + i + 1)
                at = slice(2 * P * i, 2 * P * (i + 1))
                dve.tensor_tensor(XTl[:, :, at], PS[:, i % 2, :].rearrange("p (k t) -> p k t", k=KT),
                                  XTh[:, :, at].bitcast(F32), ALU.subtract).then_inc(xt_low, 1)

            for i in range(NX):
                dve.wait_ge(x_in[i], 16)
                layernorm(i, lambda t: X[:, TPC * i + t, :], lambda t: X[:, TPC * i + t, :], xn_ready)
                if i >= 1:
                    transposed(2 * i - 2, 0)
                    transposed(2 * i - 1, 0)
            transposed(2 * NX - 2, 0)
            transposed(2 * NX - 1, 0)
            dve.wait_ge(kvw_ready, 1)
            for w in (1, 0):
                dve.tensor_tensor(Wl[:, w], Wr[:, w], Wh[:, w].bitcast(F32), ALU.subtract).then_inc(kvw_ready, 1)

            halves = [slice(0, CH), slice(CH, 2 * CH)]
            dve.wait_ge(cs_in, 16)

            def rope(i, half, stage_waits=()):
                def table(k):
                    return CS[:, k:k + 1, half].broadcast_to([P, 2, CH])

                dve.wait_ge(proj_done, i + 1)
                own.add(dve.tensor_tensor(tc[:], SD, table(0), ALU.mult))
                dve.tensor_tensor(ts[:], SD, table(1), ALU.mult).then_inc(proj_read, 1)
                dve.wait_ge(proj_read, i + 1)
                own.wait()
                own.add(dve.tensor_tensor(EO[:, 0, :], tc[:, 0, :], ts[:, 1, :], ALU.subtract))
                own.add(dve.tensor_tensor(EO[:, 1, :], tc[:, 1, :], ts[:, 0, :], ALU.add))
                own.wait()
                for s, v in stage_waits:
                    dve.wait_ge(s, v)
                own.add(dve.tensor_copy(ST[:, 0:2, half], EO[:]))
                own.wait()
                dve.tensor_tensor(ST[:, 2:4, half], EO[:], ST[:, 0:2, half].bitcast(F32), ALU.subtract
                                  ).then_inc(rope_done, 1)

            for i in range(NPROJ):
                rope(i, halves[i % 2], [(k_stored[i % 2], 16 * (i // 2))] if i >= 2 else [])
            for c in range(2):
                rope(NPROJ + c, halves[c], [(k_stored[c], 16 * NPROJ // 2)])
            dve.wait_ge(bo_in, 16)

            def normalise(n, p, c):
                m = 4 * n + 2 * p + c
                dve.wait_ge(pv_done, NU * n + PU * p + (3, PU)[c])
                pv = PV[:, :, 0:TPC * VW].rearrange("p h (t w) -> p h t w", w=VW)
                own.add(dve.reciprocal(RC[:].unsqueeze(3), pv[:, :, :, DH:DH + 1]))
                own.wait()
                if not isinstance(m, int) or m >= 1:
                    dve.wait_ge(ctxT_done, m)
                dve.tensor_tensor(CTX[:].rearrange("p t h d -> p h t d"), pv[:, :, :, 0:DH],
                                  RC[:].unsqueeze(3).broadcast_to([P, 2, TPC, DH]), ALU.mult).then_inc(norm_done, 1)

            def split_context(m):
                dve.wait_ge(ctxT_done, m + 1)
                if not isinstance(m, int) or m >= 1:
                    dve.wait_ge(y_done, 2 * m)
                src = SD[:, 0, :].rearrange("p (t s) -> p t s", t=TPC)
                own.add(dve.tensor_copy(CTh[:], src))
                own.wait()
                dve.tensor_tensor(CTl[:], src, CTh[:].bitcast(F32), ALU.subtract).then_inc(split_done, 1)

            def add_out(m, b, c, half):
                dve.wait_ge(y_done, 2 * m + half + 1)
                t = NB // B * b + TPC * c + 2 * half
                acc = yacc[:, t:t + 2, :]
                dve.tensor_tensor(acc, SD[:, 1, :].rearrange("p (t d) -> p t d", t=2), acc, ALU.add).then_inc(y_added, 1)

            def body(g, first=False, last=False):
                for b in range(B):
                    n = 2 * g + b
                    more = not (last and b == B - 1)
                    for p in range(2):
                        m = 4 * n + 2 * p
                        before = not (first and b == 0 and p == 0)
                        if p == 1 and more:
                            rope(NPROJ + 2 * n + 3, halves[1])
                        if before:
                            split_context(m - 1)
                        normalise(n, p, 0)
                        if before:
                            for half in range(2):
                                add_out(m - 1, b if p == 1 else 1 - b, 1, half)
                        split_context(m)
                        for half in range(2):
                            add_out(m, b, 0, half)
                        if p == 0 and more:
                            rope(NPROJ + 2 * n + 2, halves[0], [(qs_in[i], QT * (n + 1)) for i in range(2)])
                        normalise(n, p, 1)

            steps = B * (2 * 4 + 2 * 4)
            body(0, first=True)
            begun = own.base + own.k
            with dve.Fori(1, G - 1) as g:
                own.base, own.k = begun + steps * (g - 1), 0
                body(g)
                assert own.k == steps
            own.base, own.k = begun + steps * (G - 2), 0
            body(G - 1, last=True)
            M = 4 * B * G
            split_context(M - 1)
            for half in range(2):
                add_out(M - 1, 1, 1, half)

            dve.wait_ge(y_added, 2 * M)
            for i in range(NX):
                layernorm(NX + i, lambda t: yacc[:, TPC * i + t, :], lambda t: yacc[:, TPC * i + t, :])
                own.wait()
                if i == 0:
                    dve.wait_ge(x2_in, 16)
                c = slice(TPC * i, TPC * (i + 1))
                own.add(dve.tensor_tensor(X2[:, c, :], X2[:, c, :], yacc[:, c, :], ALU.add))
            own.wait()
            dve.wait_ge(rw_ready, 1)
            dve.tensor_tensor(Rl[:], Rr[:], Rh[:].bitcast(F32), ALU.subtract).then_inc(rw_ready, 1)
            for i in range(NX):
                layernorm(2 * NX + i, lambda t: X2[:, TPC * i + t, :], lambda t: yacc[:, TPC * i + t, :], xn_ready)
                if i >= 1:
                    transposed(2 * i - 2, NB // 2)
                    transposed(2 * i - 1, NB // 2)
            transposed(2 * NX - 2, NB // 2)
            transposed(2 * NX - 1, NB // 2)

            dve.wait_ge(lg_done, 1)
            own.add(dve.tensor_copy(LG[:], PS[:, 2, 0:16 * NB].rearrange("p (t r) -> p t r", r=16)[:, :, 0:NR]))
            own.wait()
            dve.tensor_scalar(ex[:, 1, :], LG[:, :, NE], -1.0, None, ALU.mult).then_inc(gap_ready, 1)
            for t in range(NB):
                own.add(dve.max(top[:, t, :], LG[:, t, 0:NE]))
            own.wait()
            dve.tensor_tensor(ex[:, 0, :], top[:, :, 1], top[:, :, 0], ALU.subtract).then_inc(gap_ready, 1)
            for t in range(NB):
                own.add(dve.max_index(topi[:, t, :], top[:, t, :], LG[:, t, 0:NE]))
            own.wait()
            own.add(dve.tensor_copy(topf[:], topi[:]))
            dve.wait_ge(e2_ready, 1)
            own.add(dve.tensor_scalar(den[:], ex[:], 1.0, None, ALU.add))
            own.wait()
            own.add(dve.reciprocal(wt[:, 0:2, :], den[:]))
            own.wait()
            own.add(dve.tensor_tensor(wt[:, 2, :], ex[:, 0, :], wt[:, 0, :], ALU.mult))
            own.wait()
            for e in range(NE):
                own.add(dve.scalar_tensor_tensor(out=CB[:, :, e], in0=topf[:, :, 0], scalar=float(e), in1=wt[:, 0, :],
                                                 op0=ALU.is_equal, op1=ALU.mult))
                own.add(dve.scalar_tensor_tensor(out=CB2[:, :, e], in0=topf[:, :, 1], scalar=float(e), in1=wt[:, 2, :],
                                                 op0=ALU.is_equal, op1=ALU.mult))
            own.wait()
            own.add(dve.tensor_tensor(CB[:, :, 0:NE], CB[:, :, 0:NE], CB2[:, :, 0:NE], ALU.add))
            own.add(dve.tensor_copy(CB[:, :, NE], wt[:, 1, :]))
            own.wait()
            own.add(dve.tensor_copy(CBh[:], CB[:]))
            own.wait()
            dve.tensor_copy(CBx[:, :, 0:NG], CBh[:].bitcast(F32)).then_inc(cb_ready, 1)
            dve.tensor_tensor(CBx[:, :, NG:2 * NG], CB[:], CBh[:].bitcast(F32), ALU.subtract).then_inc(cb_ready, 1)
            dve.wait_ge(ct_zero, 1)
            for i in range(NB // 4):
                dve.wait_ge(cbT_done, i + 1)
                dve.tensor_copy(CT[0:2 * NG, CH * i:CH * (i + 1)], PS[0:2 * NG, 3, :]).then_inc(cbT_read, 1)

            def low(q, j, first):
                n = NT * q + j
                dve.wait_ge(hh_done, n + 1)
                dve.wait_ge(hid_done, n + 1)
                if not first or j >= 2:
                    dve.wait_ge(down_done, n - (j > 0))
                dve.tensor_tensor(Hl[:, j % 2, :], hd[:, j % 2, :], Hh[:, j % 2, :].bitcast(F32), ALU.subtract
                                  ).then_inc(hl_done, 1)

            def chunk(q, first=False):
                for j in range(NT):
                    n = NT * q + j
                    bank = 3 * (j % 2)
                    dve.wait_ge(silu_done, n + 1)
                    if not first or j >= 2:
                        dve.wait_ge(hh_done, n - (j > 0))
                        dve.wait_ge(hl_done, n - (j > 0))
                    own.add(dve.tensor_tensor(hd[:, j % 2, :], PS[:, bank + 1, :], sg[:, j % 2, :], ALU.mult))
                    if j >= 1:
                        low(q, j - 1, first)
                    own.wait()
                    dve.tensor_tensor(hd[:, j % 2, :], PS[:, bank + 2, :], hd[:, j % 2, :], ALU.mult).then_inc(hid_done, 1)
                low(q, NT - 1, first)
                dve.wait_ge(fy_read, q + 1)
                if not first:
                    dve.wait_ge(o_out, 16 * q)
                layernorm(3 * NX + q, lambda t: Y[:, t, :], lambda t: O[:, t, :])
                own.wait()
                dve.tensor_tensor(O, O, X2[:, bass.ds(TPC * q, TPC), :], ALU.add).then_inc(o_ready, 1)

            steps = NT + 2 * TPC + 6 + TPC
            chunk(0, first=True)
            begun = own.base + own.k
            with dve.Fori(1, NX) as q:
                own.base, own.k = begun + steps * (q - 1), 0
                chunk(q)
                assert own.k == steps, own.k




def _tables():
    inv = (1.0 / 10000.0 ** (np.arange(0, DH, 2, dtype=np.float32) / DH)).astype(np.float32)
    angle = np.arange(S, dtype=np.float32)[None, :] * inv[:, None]
    cs = np.stack([np.tile(np.cos(angle), (4, 1)), np.tile(np.sin(angle), (4, 1))], 1).astype(np.float32)

    def part(v):
        m, e = np.frexp(v)
        return np.ldexp(np.round(m * 4096) / 4096, e)

    pos = np.arange(S, dtype=np.float64)
    al = np.zeros((G * 4 + R * 4, S))
    for g in range(G):
        al[4 * g:4 * g + 2] = pos * 2.0 ** -g
        al[4 * g + 2:4 * g + 4] = 2.0 ** -g
    for h in range(R):
        slope = 2.0 ** (-(h + 1) * 8.0 / H)
        rows = []
        for v in (np.full(S, slope), -slope * pos):
            rows += [part(v), part(v - part(v))]
        al[4 * G + 4 * h:4 * G + 4 * h + 4] = rows
    sel = np.zeros((2 * NG, NT * P), np.float32)
    for i in range(HID):
        e = min(i // IM, NE)
        sel[e, i] = sel[NG + e, i] = 1.0
    return cs, al.astype(np.float32), np.eye(P, dtype=np.float32), sel


def kernel(**inputs):
    import concourse.bacc as _bacc
    from concourse.bass_utils import run_bass_kernel_spmd as _run

    a = {k[3:]: np.asarray(v) for k, v in inputs.items()}
    cs, al, ident, sel = _tables()
    x = a["attn_hidden_states"].reshape(TOK, D)
    wq = a["attn_Wq"].reshape(KT, P, G, R, 32, 2).transpose(2, 1, 0, 5, 3, 4).reshape(G, P, KT, 2, P)
    wk = a["attn_Wk"].reshape(KT, P, 2, 4, 32, 2).transpose(1, 0, 2, 5, 3, 4).reshape(P, KT, CH)
    wv = a["attn_Wv"].reshape(KT, P, CH).transpose(1, 0, 2)
    wo = a["attn_Wo"].reshape(G, 2, P, D).transpose(0, 2, 1, 3)
    gu, dn = a["ffn_gate_up_proj"], a["ffn_down_proj"]
    pad = np.zeros((NT * P - HID, D), np.float32)
    gate = np.concatenate([gu[:, :IM].reshape(NE * IM, D), a["ffn_sh_gate_w"], pad])
    up = np.concatenate([gu[:, IM:].reshape(NE * IM, D), a["ffn_sh_up_w"], pad])
    down = np.concatenate([dn.transpose(0, 2, 1).reshape(NE * IM, D), a["ffn_sh_down_w"].T, pad])
    tiles = [w.reshape(NT, P, KT, P).transpose(0, 3, 2, 1).reshape(NT, P, D) for w in (gate, up)]
    wf = np.concatenate([*tiles, down.reshape(NT, P, D)], axis=2)
    wr = np.concatenate([a["ffn_router_weight"], a["ffn_shared_gate_w"], np.zeros((1, D), np.float32)])
    wr = wr.reshape(NR, KT, P).transpose(2, 1, 0)

    nc = _bacc.Bacc("TRN2", target_bir_lowering=False, num_devices=1)
    arrays, args = {}, []
    for name, v in dict(x=x, wq=wq, wk=wk, wv=wv, wo=wo, bo=a["attn_bo"], wf=wf, wr=wr, cs=cs, al=al,
                        ident=ident, sel=sel).items():
        v = np.ascontiguousarray(v)
        arrays[f"in_{name}"] = v
        args.append(nc.dram_tensor(f"in_{name}", v.shape, mybir.dt.from_np(v.dtype), kind="ExternalInput").ap())
    args.append(nc.dram_tensor("out_0", (TOK, D), F32, kind="ExternalOutput").ap())
    build(nc, *args)
    r = _run(nc, [arrays], core_ids=[0])
    return r.results[0]["out_0"].reshape(B, S, D)
```

```python
from contextlib import ExitStack

import numpy as np
import concourse.bass as bass
from concourse import mybir

F32 = mybir.dt.float32
F32R = mybir.dt.float32r
U32 = mybir.dt.uint32
ALU = mybir.AluOpType
ACT = mybir.ActivationFunctionType

P = 128
B, S, D = 2, 1024, 256
TOK = B * S
NB = TOK // P
H, G, DH = 32, 8, 64
R = H // G
KT = D // P
CH = 512
NE, IM, ISH = 8, 176, 704
HID = NE * IM + ISH
NT = -(-HID // P)
NG = NE + 1
NH = 3
EPS = 1e-5
CAP = 30.0
VW = DH + 2
VN = 128
TPC = CH // P



def unit_pieces(u):
    def diagonal(hh, c):
        return [(hh, 4 * c, CH * c, CH, 0), (hh, 4 * c + 3, CH * c + 384, 128, CH),
                (hh, 4 * c + 1, CH * c + 128, 384, CH + 128)]

    def rest(c):
        return [(hh, 4 * c + 2, CH * c + 256, 256, 256 * hh) for hh in range(2)]

    def full(hh, t):
        return [(hh, t, CH, CH, 0), (hh, t + 1, CH, CH, CH)]

    return [diagonal(0, 0), diagonal(1, 0), rest(0), full(0, 0), full(0, 2), diagonal(0, 1),
            full(1, 0), full(1, 2), diagonal(1, 1), rest(1)][u]


AHEAD = 4
NP = 5
PU = 10
NU = 2 * PU
WIDTH = [sum(p[3] for p in unit_pieces(u)) for u in range(PU)]
MASKED = [u for u in range(PU) if u not in (3, 4, 6, 7)]
NM = 2 * len(MASKED)
CHUNK_END = {2: 0, 9: 1}
CHUNK_START = {0: 0, 3: 1}


def masked_count(n, u):
    p, v = divmod(u, PU)
    return NM * n + len(MASKED) * p + MASKED.index(v) + 1


def wait_apart(eng, sem, value, passed):
    eng.wait_ge(sem, value)
    if not isinstance(value, int):
        eng.sem_inc(passed, 1)


class Steps:

    def __init__(self, eng, sem):
        self.eng, self.sem, self.base, self.k = eng, sem, 0, 0

    def add(self, instruction):
        instruction.then_inc(self.sem, 1)
        self.k += 1
        return self.k

    def wait(self, k=None):
        self.eng.wait_ge(self.sem, self.base + (self.k if k is None else k))

    def wait_apart(self, passed):
        wait_apart(self.eng, self.sem, self.base + self.k, passed)


def build(nc, x, wq, wk, wv, wo, bo, wf, wr, cs, al, ident, sel, out):
    with ExitStack() as ctx:
        def sem(name):
            return ctx.enter_context(nc.semaphore(name))

        def sb(stack, name, shape, dt=F32):
            return stack.enter_context(nc.sbuf_tensor(name, shape, dt))

        ks_dram = nc.dram_tensor("ks_scratch", (4, G * 32, TOK), F32, kind="Internal").ap()
        ka_dram = nc.dram_tensor("ka_scratch", (G * 4, S), F32, kind="Internal").ap()

        PS = ctx.enter_context(nc.psum_tensor("PS", [P, 8, CH], F32))
        SC = PS[:, 0:4, :].rearrange("p (b k) n -> p b (k n)", b=2)
        PV = PS[:, 4:6, :]
        SD = PS[:, 6:8, :]

        XTh = sb(ctx, "XTh", [P, KT, TOK], F32R)
        XTl = sb(ctx, "XTl", [P, KT, TOK], F32R)
        yacc = sb(ctx, "yacc", [P, NB, D])
        idn = sb(ctx, "idn", [P, P])
        stats = sb(ctx, "stats", [P, NB, 6])
        mv = sb(ctx, "mv", [P, NB, 2])
        vareps = sb(ctx, "vareps", [P, NB])
        std = sb(ctx, "std", [P, NB])
        rstd = sb(ctx, "rstd", [P, NB])
        newton = sb(ctx, "newton", [P, NB])
        nbias = sb(ctx, "nbias", [P, NB])

        att = ExitStack()
        KKa = [sb(att, f"KKa{b}", [P, S], F32R) for b in range(B)]
        KKb = [sb(att, f"KKb{b}", [P, S], F32R) for b in range(B)]
        ST = sb(att, "ST", [P, 4, S], F32R)
        tc = sb(att, "tc", [P, 2, CH])
        ts = sb(att, "ts", [P, 2, CH])
        EO = sb(att, "EO", [P, 2, CH])
        CS = sb(att, "CS", [P, 2, S])
        Vflat = sb(att, "Vflat", [P, NB * G * VW + VN - VW])
        V = Vflat[:, 0:NB * G * VW].rearrange("p (t g w) -> p t g w", t=NB, g=G)
        WQr = sb(att, "WQr", [P, KT, 2, P])
        WQh = sb(att, "WQh", [P, KT, 2, P], F32R)
        WQl = sb(att, "WQl", [P, KT, 2, P], F32R)
        WOr = sb(att, "WOr", [P, 2, D])
        WOh = sb(att, "WOh", [P, 2, D], F32R)
        WOl = sb(att, "WOl", [P, 2, D], F32R)
        CTX = [sb(att, f"CTX{c}", [P, TPC, 2, DH]) for c in range(2)]
        RC = sb(att, "RC", [P, 2, TPC])
        CTh = sb(att, "CTh", [P, TPC, P], F32R)
        CTl = sb(att, "CTl", [P, TPC, P], F32R)
        pro = ExitStack()
        X = sb(pro, "X", [P, NB, D])
        Wr = sb(pro, "Wr", [P, 2, KT, CH])
        Wh = sb(pro, "Wh", [P, 2, KT, CH], F32R)
        Wl = sb(pro, "Wl", [P, 2, KT, CH], F32R)
        ALr = sb(pro, "ALr", [48, S])
        pro.close()
        QSa = sb(att, "QSa", [P, R, S], F32R)
        QSb = sb(att, "QSb", [P, R, S], F32R)
        with ExitStack() as early:
            ALh = sb(early, "ALh", [48, S], F32R)
        PR = sb(att, "PR", [P, NP, 2 * CH])
        att.close()

        ffn = ExitStack()
        X2 = sb(ffn, "X2", [P, NB, D])
        CT = sb(ffn, "CT", [P, TOK], F32R)
        SL = sb(ffn, "SL", [P, NT * P], F32R)
        WFr = sb(ffn, "WFr", [P, 2, 3 * D])
        WFh = sb(ffn, "WFh", [P, NT, 3 * D], F32R)
        router = ExitStack()
        SLr = sb(router, "SLr", [P, NT * P])
        router.close()
        WFl = sb(ffn, "WFl", [P, NT, 3 * D], F32R)
        router = ExitStack()
        Rr = sb(router, "Rr", [P, KT, P])
        Rh = sb(router, "Rh", [P, KT, P], F32R)
        Rl = sb(router, "Rl", [P, KT, P], F32R)
        LG = sb(router, "LG", [P, NB, NG])
        top = sb(router, "top", [P, NB, 8])
        topi = sb(router, "topi", [P, NB, 8], U32)
        topf = sb(router, "topf", [P, NB, 8])
        ex = sb(router, "ex", [P, 2, NB])
        den = sb(router, "den", [P, 2, NB])
        wt = sb(router, "wt", [P, 3, NB])
        CB = sb(router, "CB", [P, NB, NG])
        CB2 = sb(router, "CB2", [P, NB, NG])
        CBh = sb(router, "CBh", [P, NB, NG], F32R)
        CBx = sb(router, "CBx", [P, NB, 2 * NG])
        router.close()
        Hh = sb(ffn, "Hh", [P, NH, CH], F32R)
        Hl = sb(ffn, "Hl", [P, NH, CH], F32R)
        ffn.close()
        sg, hd, Y, O = (yacc[:, 4 * i:4 * i + 4, :].rearrange("p (a b) d -> p a (b d)", a=2) for i in range(4))
        Y, O = (t.rearrange("p a (b d) -> p (a b) d", b=2) for t in (Y, O))
        LT = yacc[0:NG, NB // 2:NB, :].rearrange("p t d -> p (t d)")

        NX = NB // TPC
        x_in = [sem(f"x_in{i}") for i in range(NX)]
        kv_in, cs_in, id_in, al_in, bo_in, q_in, o_in = (sem(n) for n in
            ("kv_in", "cs_in", "id_in", "al_in", "bo_in", "q_in", "o_in"))
        dve_step, pool_step = sem("dve_step"), sem("pool_step")
        dve_passed, pool_passed = sem("dve_passed"), sem("pool_passed")
        var_ready, std_ready, ln_ready, xn_ready, yn_ready, fn_ready = (sem(n) for n in
            ("var_ready", "std_ready", "ln_ready", "xn_ready", "yn_ready", "fn_ready"))
        xt_psum, xt_high, xt_low = sem("xt_psum"), sem("xt_high"), sem("xt_low")
        kvw_ready = sem("kvw_ready")
        v_psum, v_ready, v_ones = sem("v_psum"), sem("v_ready"), sem("v_ones")
        al_ready, ka_stored, slope_rows = sem("al_ready"), sem("ka_stored"), sem("slope_rows")
        k_stored = [sem(f"k_stored{i}") for i in range(2)]
        kk_in = [sem(f"kk_in{b}") for b in range(B)]
        qs_in = [sem(f"qs_in{p}") for p in range(2)]
        proj_done, proj_read, rope_done = sem("proj_done"), sem("proj_read"), sem("rope_done")
        wq_ready, wo_ready = sem("wq_ready"), sem("wo_ready")
        qk_done, tanh_done, exp_done, mask_done, pv_done = (sem(n) for n in
            ("qk_done", "tanh_done", "exp_done", "mask_done", "pv_done"))
        norm_done, ctxT_done, split_done, y_done, y_added = (sem(n) for n in
            ("norm_done", "ctxT_done", "split_done", "y_done", "y_added"))
        x2_in = sem("x2_in")
        r_in, rw_ready, lt_done, lt_read, lg_done, cb_ready, cbT_done, cbT_read, ct_zero = (sem(n) for n in
            ("r_in", "rw_ready", "lt_done", "lt_read", "lg_done", "cb_ready", "cbT_done", "cbT_read", "ct_zero"))
        gap_ready, e2_ready, sel_zero, sel_in, sel_ready = (sem(n) for n in
            ("gap_ready", "e2_ready", "sel_zero", "sel_in", "sel_ready"))
        wf_in = [sem(f"wf_in{i}") for i in range(2)]
        wfh_ready, wfl_ready = sem("wfh_ready"), sem("wfl_ready")
        guc_done, silu_done, hid_done, hh_done, hl_done, down_done = (sem(n) for n in
            ("guc_done", "silu_done", "hid_done", "hh_done", "hl_done", "down_done"))
        fy_done, fy_read, o_ready, o_out = (sem(n) for n in ("fy_done", "fy_read", "o_ready", "o_out"))

        NPROJ = 8
        QT = 16 * 12
        KL = 16 * 7

        block = ctx.enter_context(nc.Block())

        @block.sync
        def _(sp):
            xv = x.rearrange("(q t p) d -> q p t d", p=P, t=TPC)
            for i in range(NX):
                sp.dma_start(X[:, TPC * i:TPC * (i + 1), :], xv[i]).then_inc(x_in[i], 16)
                if i == 0:
                    sp.dma_start(idn[:], ident).then_inc(id_in, 16)
            sp.dma_start(Wr[:, 1], wv).then_inc(kv_in, 16)
            sp.dma_start(Wr[:, 0], wk).then_inc(kv_in, 16)
            sp.dma_start(CS[:], cs).then_inc(cs_in, 16)
            sp.dma_start(WQr[:], wq[0]).then_inc(q_in, 16)
            sp.dma_start(WOr[:], wo[0]).then_inc(o_in, 16)
            sp.dma_start(ALr[:], al).then_inc(al_in, 16)
            sp.dma_start(yacc[:], bo.partition_broadcast(P).unsqueeze(1).broadcast_to([P, NB, D])
                         ).then_inc(bo_in, 16)
            for i in range(NPROJ):
                s, q = divmod(i, 4)
                sp.wait_ge(rope_done, i + 1)
                sp.dma_start(ks_dram[:, P * s:P * (s + 1), CH * q:CH * (q + 1)].rearrange("k p n -> p k n"),
                             ST[:, :, CH * (i % 2):CH * (i % 2 + 1)].bitcast(F32)).then_inc(k_stored[i % 2], 16)
            sp.wait_ge(al_ready, 1)
            sp.dma_start(ka_dram, ALh[0:32, :].bitcast(F32)).then_inc(ka_stored, 16)
            for h in range(R):
                sp.dma_start(QSb[64:68, h, :].bitcast(F32), ALh[32 + 4 * h:36 + 4 * h, :].bitcast(F32)).then_inc(slope_rows, 16)
            for i in range(2):
                sp.wait_ge(k_stored[i], 16 * NPROJ // 2)
            sp.wait_ge(ka_stored, 16)

            def load_keys(g, b):
                for quarter in range(4):
                    sp.dma_start(KKa[b][32 * quarter:32 * quarter + 32, :].bitcast(F32),
                                 ks_dram[quarter % 2, bass.ds(32 * g, 32), S * b:S * (b + 1)]).then_inc(kk_in[b], 16)
                for quarter in range(2):
                    sp.dma_start(KKb[b][32 * quarter:32 * quarter + 32, :].bitcast(F32),
                                 ks_dram[2 + quarter, bass.ds(32 * g, 32), S * b:S * (b + 1)]).then_inc(kk_in[b], 16)
                sp.dma_start(KKb[b][64:68, :].bitcast(F32), ka_dram[bass.ds(4 * g, 4), :]).then_inc(kk_in[b], 16)

            def move_queries(p):
                for h in (2 * p, 2 * p + 1):
                    for kind in range(4):
                        sp.dma_start(QSa[32 * kind:32 * kind + 32, h, :].bitcast(F32),
                                     ST[32 * h:32 * h + 32, kind, :].bitcast(F32)).then_inc(qs_in[p], 16)
                    for kind in range(2):
                        sp.dma_start(QSb[32 * kind:32 * kind + 32, h, :].bitcast(F32),
                                     ST[32 * h:32 * h + 32, kind, :].bitcast(F32)).then_inc(qs_in[p], 16)

            load_keys(0, 0)
            sp.wait_ge(rope_done, NPROJ + 2)
            move_queries(0)
            move_queries(1)
            load_keys(0, 1)

            def body(g, last=False):
                for b in range(B):
                    n = 2 * g + b
                    if not last:
                        if b == 0:
                            sp.wait_ge(wq_ready, g + 1)
                            sp.dma_start(WQr[:], wq[bass.ds(g + 1, 1)].squeeze(0)).then_inc(q_in, 16)
                        else:
                            sp.wait_ge(wo_ready, g + 1)
                            sp.dma_start(WOr[:], wo[bass.ds(g + 1, 1)].squeeze(0)).then_inc(o_in, 16)
                    if not (last and b == B - 1):
                        sp.wait_ge(rope_done, NPROJ + 2 * n + 4)
                        sp.wait_ge(qk_done, NU * n + PU)
                        move_queries(0)
                        sp.wait_ge(qk_done, NU * n + NU)
                        move_queries(1)
                        if not last:
                            load_keys(g + 1, b)

            body(0)
            with sp.Fori(1, G - 1) as g:
                body(g)
            body(G - 1, last=True)

            sp.wait_ge(y_added, 2 * 4 * B * G)
            sp.dma_start(X2[:], x.rearrange("(t p) d -> p t d", p=P)).then_inc(x2_in, 16)
            sp.dma_start(Rr[:], wr).then_inc(r_in, 16)
            sp.wait_ge(sel_zero, 1)
            sp.dma_start(SLr[0:2 * NG, :], sel).then_inc(sel_in, 16)
            for j in range(NT):
                if j >= 2:
                    sp.wait_ge(wfl_ready, j - 1)
                sp.dma_start(WFr[:, j % 2], wf[j]).then_inc(wf_in[j % 2], 16)
            ov = out.rearrange("(q t p) d -> q p t d", p=P, t=TPC)
            with sp.Fori(0, NX) as q:
                sp.wait_ge(o_ready, q + 1)
                sp.dma_start(ov[bass.ds(q, 1)].squeeze(0), O[:]).then_inc(o_out, 16)
            sp.wait_ge(o_out, 16 * NX)

        @block.tensor
        def _(pe):
            def three(dst, ah, al_, bh, bl, kts, first=True, last=True, **kw):
                terms = [(a(k), b(k)) for k in kts for a, b in ((ah, bh), (ah, bl), (al_, bh))]
                for i, (a, b) in enumerate(terms):
                    mm = pe.matmul(dst, a, b, start=first and i == 0, stop=last and i == len(terms) - 1, **kw)
                return mm

            pe.wait_ge(id_in, 16)
            for i in range(NB // 2):
                pe.wait_ge(xn_ready, 2 * i + 2)
                if i >= 2:
                    pe.wait_ge(xt_high, i - 1)
                    pe.wait_ge(xt_low, i - 1)
                dst = PS[:, i % 2, :].rearrange("p (k t) -> p k t", k=KT)
                for t in range(2):
                    for k in range(KT):
                        mm = pe.transpose(dst[:, k, P * t:P * (t + 1)], X[:, 2 * i + t, P * k:P * (k + 1)], idn[:])
                mm.then_inc(xt_psum, 1)
            pe.wait_ge(xt_high, NB // 2)
            pe.wait_ge(xt_low, NB // 2)
            pe.wait_ge(kvw_ready, 3)
            def project(w_hi, w_lo, tokens, i):
                if not isinstance(i, int) or i >= 1:
                    pe.wait_ge(proj_read, i)
                for eo in range(2):
                    mm = three(SD[:, eo, :], lambda k: w_hi(k, eo), lambda k: w_lo(k, eo),
                               lambda k: XTh[:, k, tokens], lambda k: XTl[:, k, tokens], range(KT))
                mm.then_inc(proj_done, 1)

            def values(t):
                if t >= 4:
                    pe.wait_ge(v_ready, t - 3)
                tok = slice(P * t, P * (t + 1))
                three(PS[:, 2 + t % 4, :], lambda k: XTh[:, k, tok], lambda k: XTl[:, k, tok],
                      lambda k: Wh[:, 1, k, :], lambda k: Wl[:, 1, k, :], range(KT)).then_inc(v_psum, 1)

            for i in range(NPROJ):
                s, q = divmod(i, 4)
                project(lambda k, eo: Wh[:, 0, k, 256 * s + P * eo:256 * s + P * (eo + 1)],
                        lambda k, eo: Wl[:, 0, k, 256 * s + P * eo:256 * s + P * (eo + 1)],
                        slice(CH * q, CH * (q + 1)), i)
                values(2 * i)
                values(2 * i + 1)

            def queries(n, b, c):
                project(lambda k, eo: WQh[:, k, eo, :], lambda k, eo: WQl[:, k, eo, :],
                        slice(S * b + CH * c, S * b + CH * (c + 1)), NPROJ + 2 * n + c)

            pe.wait_ge(wq_ready, 1)
            queries(0, 0, 0)
            queries(0, 0, 1)
            pe.wait_ge(v_ready, NB)
            pe.wait_ge(v_ones, 2)
            pe.wait_ge(slope_rows, 16 * R)

            def scores(n, g, b, u):
                p, v = divmod(u, PU)
                if u == 0:
                    pe.wait_ge(kk_in[b], KL * (g + 1))
                if v == 0:
                    pe.wait_ge(qs_in[p], QT * (n + 1))
                U = NU * n + u
                if not isinstance(U, int) or U >= 2:
                    pe.wait_ge(tanh_done, U - 1)
                for hh, t, s0, w, col in unit_pieces(v):
                    dst = SC[:, u % 2, col:col + w]
                    keys, q = slice(P * t, P * (t + 1)), slice(s0, s0 + w)
                    pe.matmul(dst, KKa[b][:, keys], QSa[:, 2 * p + hh, q], start=True, stop=False)
                    mm = pe.matmul(dst, KKb[b][0:68, keys], QSb[0:68, 2 * p + hh, q], start=False, stop=True)
                mm.then_inc(qk_done, 1)

            def context(n, g, b, u):
                p, v = divmod(u, PU)
                if v in MASKED:
                    pe.wait_ge(mask_done, masked_count(n, u))
                else:
                    pe.wait_ge(exp_done, NU * n + u + 1)
                if v in CHUNK_START:
                    m = 4 * n + 2 * p + CHUNK_START[v]
                    if not isinstance(m, int) or m >= 1:
                        pe.wait_ge(norm_done, m)
                started = {0: v not in (0, 3), 1: v not in (1, 6)}
                pieces = unit_pieces(v)
                for i, (hh, t, s0, w, col) in enumerate(pieces):
                    for k in range(w // P):
                        blk = (s0 // P + k) % TPC
                        mm = pe.matmul(PV[:, hh, VN * blk:VN * (blk + 1)],
                                       PR[:, u % NP, col + P * k:col + P * (k + 1)],
                                       Vflat[:, bass.ds(VW * (G * (NB // B * b + t) + g), VN)],
                                       start=not started[hh], stop=v in CHUNK_END and k == w // P - 1,
                                       skip_group_check=True)
                        started[hh] = True
                mm.then_inc(pv_done, 1)

            def turn(m, c, projections):
                pe.wait_ge(norm_done, m + 1)
                pe.wait_ge(proj_read, projections)
                if not isinstance(m, int) or m >= 1:
                    pe.wait_ge(split_done, m)
                for k in range(TPC):
                    mm = pe.transpose(SD[:, 0, P * k:P * (k + 1)], CTX[c][:, k, :, :].rearrange("p h d -> p (h d)"), idn[:])
                mm.then_inc(ctxT_done, 1)

            def project_out(m, p, half):
                if half == 0:
                    pe.wait_ge(split_done, m + 1)
                if not isinstance(m, int) or 2 * m + half >= 1:
                    pe.wait_ge(y_added, 2 * m + half)
                for i in range(2):
                    k = 2 * half + i
                    mm = three(SD[:, 1, D * i:D * (i + 1)], lambda _: CTh[:, k, :], lambda _: CTl[:, k, :],
                               lambda _: WOh[:, p, :], lambda _: WOl[:, p, :], [0])
                mm.then_inc(y_done, 1)

            def side(n, g, b, u, first, last):
                p, v = divmod(u, PU)
                m = 4 * n + 2 * p
                before = not (first and b == 0 and p == 0)
                more = not (last and b == B - 1)
                if more and p == 0 and v in (3, 9):
                    if b == B - 1 and v == 3:
                        pe.wait_ge(wq_ready, g + 2)
                    outs = m if v == 3 else m + 1
                    if before or v == 9:
                        pe.wait_ge(split_done, outs)
                        pe.wait_ge(y_added, 2 * outs)
                    queries(n + 1, (b + 1) % B, v // 9)
                projections = NPROJ + 2 * n + 2
                if more:
                    projections += 2 if p == 1 else int(v > 3)
                if v == p and before:
                    turn(m - 1, 1, projections)
                if v in (p + 1, p + 2) and before:
                    project_out(m - 1, 1 - p, v - p - 1)
                if v == 5 + p:
                    turn(m, 0, projections)
                if v in (7 + p, 8 + p):
                    if v == 7 and b == 0 and p == 0:
                        pe.wait_ge(wo_ready, g + 1)
                    project_out(m, p, v - 7 - p)

            def body(g, first=False, last=False):
                for b in range(B):
                    n = 2 * g + b
                    for u in range(NU):
                        if u + AHEAD < NU:
                            scores(n, g, b, u + AHEAD)
                        elif b == 0:
                            scores(n + 1, g, 1, u + AHEAD - NU)
                        elif not last:
                            scores(n + 1, g + 1, 0, u + AHEAD - NU)
                        context(n, g, b, u)
                        side(n, g, b, u, first, last)

            for u in range(AHEAD):
                scores(0, 0, 0, u)
            body(0, first=True)
            with pe.Fori(1, G - 1) as g:
                body(g)
            body(G - 1, last=True)
            M = 4 * B * G
            turn(M - 1, 1, NPROJ + 2 * B * G)
            project_out(M - 1, 1, 0)
            project_out(M - 1, 1, 1)

            for i in range(NB // 2):
                pe.wait_ge(xn_ready, NB + 2 * i + 2)
                if i >= 2:
                    pe.wait_ge(xt_high, NB // 2 + i - 1)
                    pe.wait_ge(xt_low, NB // 2 + i - 1)
                dst = PS[:, i % 2, :].rearrange("p (k t) -> p k t", k=KT)
                for t in range(2):
                    for k in range(KT):
                        mm = pe.transpose(dst[:, k, P * t:P * (t + 1)], yacc[:, 2 * i + t, P * k:P * (k + 1)], idn[:])
                mm.then_inc(xt_psum, 1)
            pe.wait_ge(xt_high, NB)
            pe.wait_ge(xt_low, NB)
            pe.wait_ge(rw_ready, 2)
            for i in range(NX):
                tok = slice(CH * i, CH * (i + 1))
                three(PS[:, 2 + i, :], lambda k: Rh[:, k, :], lambda k: Rl[:, k, :],
                      lambda k: XTh[:, k, tok], lambda k: XTl[:, k, tok], range(KT)).then_inc(lt_done, 1)
            for t in range(NB):
                pe.wait_ge(lt_read, t // TPC + 1)
                mm = pe.transpose(PS[:, 6, 16 * t:16 * t + NG], LT[:, P * t:P * (t + 1)], idn[0:NG, 0:NG])
            mm.then_inc(lg_done, 1)

            def gate_up(q, j):
                if not isinstance(q, int) or q >= 1:
                    pe.wait_ge(hid_done, NT * q + j - (j > 0))
                elif j >= 2:
                    pe.wait_ge(hid_done, j - 1)
                tok = bass.ds(CH * q, CH)
                for part in range(2):
                    three(PS[:, 3 * (j % 2) + part, :], lambda k: WFh[:, j, 256 * part + P * k:256 * part + P * (k + 1)],
                          lambda k: WFl[:, j, 256 * part + P * k:256 * part + P * (k + 1)],
                          lambda k: XTh[:, k, tok], lambda k: XTl[:, k, tok], range(KT))
                pe.matmul(PS[:, 3 * (j % 2) + 2, :], SL[:, P * j:P * (j + 1)], CT[:, tok], start=True, stop=True
                          ).then_inc(guc_done, 1)

            def down(q, j):
                pe.wait_ge(hh_done, NT * q + j + 1)
                pe.wait_ge(hl_done, NT * q + j + 1)
                if j == 0 and (not isinstance(q, int) or q >= 1):
                    pe.wait_ge(fy_read, q)
                for t in range(TPC):
                    tok = slice(P * t, P * (t + 1))
                    w = slice(2 * D, 3 * D)
                    dst = PS[:, 6 + t // 2, D * (t % 2):D * (t % 2 + 1)]
                    for i, (a, w_) in enumerate(((Hh, WFh), (Hh, WFl), (Hl, WFh))):
                        mm = pe.matmul(dst, a[:, j % NH, tok], w_[:, j, w], start=j == 0 and i == 0 and t % 2 == 0,
                                       stop=j == NT - 1 and i == 2, skip_group_check=True)
                mm.then_inc(down_done, 1)

            def chunk(q, first=False):
                for j in range(NT + 2):
                    if j < NT:
                        if first:
                            pe.wait_ge(wfh_ready, j + 1)
                            pe.wait_ge(wfl_ready, j + 1)
                        gate_up(q, j)
                    if j >= 2:
                        down(q, j - 2)

            pe.wait_ge(cb_ready, 2)
            for i in range(NX):
                for t in range(TPC):
                    mm = pe.transpose(PS[0:2 * NG, 2 + i, P * t:P * (t + 1)], CBx[:, TPC * i + t, :], idn[:])
                mm.then_inc(cbT_done, 1)
            pe.wait_ge(cbT_read, NB // 4)
            pe.wait_ge(sel_ready, 1)
            pe.wait_ge(ct_zero, 1)
            chunk(0, first=True)
            with pe.Fori(1, NX) as q:
                chunk(q)

        @block.scalar
        def _(act):
            def roots(i):
                act.wait_ge(var_ready, i + 1)
                act.activation(std[:, TPC * (i % NX):TPC * (i % NX + 1)], vareps[:, TPC * (i % NX):TPC * (i % NX + 1)],
                               ACT.Sqrt).then_inc(std_ready, 1)

            def normalised(i, src, dst, signal):
                act.wait_ge(ln_ready, i + 1)
                for t in range(TPC):
                    b = TPC * (i % NX if isinstance(i, int) and i < 3 * NX else 0) + t
                    act.activation(dst(t), src(t), ACT.Identity, bias=nbias[:, b:b + 1], scale=rstd[:, b:b + 1]
                                   ).then_inc(signal, 1)

            def expert_weights(j):
                act.wait_ge(wf_in[j % 2], 16 * (j // 2 + 1))
                act.copy(WFh[:, j, :], WFr[:, j % 2, :]).then_inc(wfh_ready, 1)

            def transposed(i, total):
                act.wait_ge(xt_psum, total + i + 1)
                act.copy(XTh[:, :, 2 * P * i:2 * P * (i + 1)], PS[:, i % 2, :].rearrange("p (k t) -> p k t", k=KT)
                         ).then_inc(xt_high, 1)

            roots(0)
            for i in range(NX):
                if i + 1 < NX:
                    roots(i + 1)
                block_of = lambda t: X[:, TPC * i + t, :]
                normalised(i, block_of, block_of, xn_ready)
                if i == 0:
                    act.wait_ge(kv_in, 32)
                    act.copy(Wh[:], Wr[:]).then_inc(kvw_ready, 1)
                if i >= 1:
                    transposed(2 * i - 2, 0)
                    transposed(2 * i - 1, 0)
            transposed(2 * NX - 2, 0)
            transposed(2 * NX - 1, 0)
            for t in range(NB):
                act.wait_ge(v_psum, t + 1)
                act.copy(V[:, t, :, 0:DH], PS[:, 2 + t % 4, :].rearrange("p (g d) -> p g d", g=G)).then_inc(v_ready, 1)
            act.wait_ge(al_in, 16)
            act.wait_ge(proj_done, NPROJ + 1)
            act.copy(ALh[:], ALr[:]).then_inc(al_ready, 1)

            def capped(n, u):
                U = NU * n + u
                act.wait_ge(qk_done, U + 1)
                if not isinstance(U, int) or U >= NP:
                    act.wait_ge(pv_done, U - NP + 1)
                w = WIDTH[u % PU]
                act.activation(PR[:, u % NP, 0:w], SC[:, u % 2, 0:w], ACT.Tanh, scale=1.0 / (CAP * DH ** 0.5)
                               ).then_inc(tanh_done, 1)

            def exponential(n, u):
                act.wait_ge(tanh_done, NU * n + u + 1)
                w = WIDTH[u % PU]
                act.activation(PR[:, u % NP, 0:w], PR[:, u % NP, 0:w], ACT.Exp, scale=CAP).then_inc(exp_done, 1)

            def body(g, last=False):
                for b in range(B):
                    n = 2 * g + b
                    for u in range(NU):
                        if u + 1 < NU:
                            capped(n, u + 1)
                        elif not (last and b == B - 1):
                            capped(n + 1, 0)
                        exponential(n, u)

            capped(0, 0)
            body(0)
            with act.Fori(1, G - 1) as g:
                body(g)
            body(G - 1, last=True)

            roots(NX)
            for k in range(NX, 3 * NX):
                i = k % NX
                if k + 1 < 3 * NX:
                    roots(k + 1)
                to = lambda t: yacc[:, TPC * i + t, :]
                if k < 2 * NX:
                    normalised(k, to, to, yn_ready)
                else:
                    normalised(k, lambda t: X2[:, TPC * i + t, :], to, xn_ready)
                if k == NX:
                    act.wait_ge(r_in, 16)
                    act.copy(Rh[:], Rr[:]).then_inc(rw_ready, 1)
                    act.wait_ge(sel_in, 16)
                    act.copy(SL[:], SLr[:]).then_inc(sel_ready, 1)
                    expert_weights(0)
                    expert_weights(1)
                if k > 2 * NX:
                    transposed(2 * i - 2, NB // 2)
                    transposed(2 * i - 1, NB // 2)
            transposed(2 * NX - 2, NB // 2)
            transposed(2 * NX - 1, NB // 2)
            for i in range(NX):
                act.wait_ge(lt_done, i + 1)
                act.copy(LT[:, CH * i:CH * (i + 1)], PS[0:NG, 2 + i, :]).then_inc(lt_read, 1)
            act.wait_ge(gap_ready, 2)
            act.activation(ex[:], ex[:], ACT.Exp).then_inc(e2_ready, 1)

            def chunk(q, first=False):
                for j in range(NT):
                    if first and j + 2 < NT:
                        expert_weights(j + 2)
                    n = NT * q + j
                    act.wait_ge(guc_done, n + 1)
                    if not first or j >= 2:
                        act.wait_ge(hid_done, n - (j > 0))
                    act.activation(sg[:, j % 2, :], PS[:, 3 * (j % 2), :], ACT.Silu).then_inc(silu_done, 1)
                    act.wait_ge(hid_done, n + 1)
                    if not first or j >= NH:
                        act.wait_ge(down_done, n - (1 if j < 2 else 2))
                        act.wait_ge(hl_done, n - (1 if j < 2 else 2))
                    act.copy(Hh[:, j % NH, :], hd[:, j % 2, :]).then_inc(hh_done, 1)
                    if not first and j == 2:
                        root(3 * NX + q - 1)
                    if not first and j == 4:
                        output_norm(q - 1)
                act.wait_ge(down_done, NT * q + NT)
                act.copy(Y, PS[:, 6:8, :].rearrange("p b (t d) -> p (b t) d", t=2)).then_inc(fy_read, 1)

            def root(i):
                act.wait_ge(var_ready, i + 1)
                act.activation(std[:, 0:TPC], vareps[:, 0:TPC], ACT.Sqrt).then_inc(std_ready, 1)

            def output_norm(q):
                if not isinstance(q, int) or q >= 1:
                    act.wait_ge(o_out, 16 * q)
                normalised(3 * NX + q, lambda t: Y[:, t, :], lambda t: O[:, t, :], fn_ready)

            chunk(0, first=True)
            with act.Fori(1, NX) as q:
                chunk(q)
            root(4 * NX - 1)
            output_norm(NX - 1)

        @block.gpsimd
        def _(pool):
            own = Steps(pool, pool_step)
            pool.memset(V[:, :, :, DH:VW], 1.0).then_inc(v_ones, 1)
            pool.memset(Vflat[:, NB * G * VW:], 0.0).then_inc(v_ones, 1)

            def split(raw, hi, lo, ready):
                own.add(pool.tensor_copy(hi[:], raw[:]))
                own.wait()
                pool.tensor_tensor(lo[:], raw[:], hi[:].bitcast(F32), ALU.subtract).then_inc(ready, 1)

            pool.wait_ge(q_in, 16)
            split(WQr, WQh, WQl, wq_ready)

            def body(g, last=False):
                for b in range(B):
                    n = 2 * g + b
                    for u in range(NU):
                        p, v = divmod(u, PU)
                        if v not in MASKED:
                            continue
                        wait_apart(pool, exp_done, NU * n + u + 1, pool_passed)
                        if v in CHUNK_END:
                            spots = [PR[:, u % NP, 0:CH].rearrange("p (a s) -> p a s", a=2)[:, :, 0:P]]
                        else:
                            spots = [PR[:, u % NP, 0:P].unsqueeze(1),
                                     PR[:, u % NP, CH:CH + 2 * P].rearrange("p (a s) -> p a s", a=2)]
                        for spot in spots:
                            done = pool.affine_select(out=spot, in_=spot, compare_op=ALU.is_ge, fill=0.0, base=0,
                                                      pattern=[[0, spot.shape[1]], [1, P]], channel_multiplier=-1)
                        done.then_inc(mask_done, 1)
                        if u == 5 and b == 0:
                            if not isinstance(g, int) or g >= 1:
                                wait_apart(pool, y_done, 16 * g, pool_passed)
                            wait_apart(pool, o_in, 16 * (g + 1), pool_passed)
                            split(WOr, WOh, WOl, wo_ready)
                        if u == PU + 5 and b == 0 and not last:
                            wait_apart(pool, q_in, 16 * (g + 2), pool_passed)
                            wait_apart(pool, proj_done, NPROJ + 4 * g + 4, pool_passed)
                            split(WQr, WQh, WQl, wq_ready)

            body(0)
            per = own.k - 1
            with pool.Fori(1, G - 1) as g:
                own.base, own.k = 1 + per * g, 0
                body(g)
            own.base, own.k = 1 + per * (G - 1), 0
            body(G - 1, last=True)
            pool.wait_ge(y_done, 2 * 4 * B * G)
            pool.wait_ge(y_added, 2 * 4 * B * G)
            pool.memset(SLr[:], 0.0).then_inc(sel_zero, 1)
            pool.memset(CT[:].bitcast(F32), 0.0).then_inc(ct_zero, 1)
            pool.wait_ge(sel_ready, 1)
            for j in range(NT):
                pool.wait_ge(wfh_ready, j + 1)
                pool.tensor_tensor(WFl[:, j, :], WFr[:, j % 2, :], WFh[:, j, :].bitcast(F32), ALU.subtract
                                   ).then_inc(wfl_ready, 1)

        @block.vector
        def _(dve):
            own = Steps(dve, dve_step)

            def ln_stats(i, src, slot):
                c = slice(TPC * slot, TPC * (slot + 1))
                for t in range(TPC):
                    own.add(dve.bn_stats(stats[:, TPC * slot + t, :], src(t)))
                own.wait_apart(dve_passed)
                for t in range(TPC):
                    own.add(dve.bn_aggr(mv[:, TPC * slot + t, :], stats[:, TPC * slot + t, :]))
                own.wait()
                dve.tensor_scalar(vareps[:, c], mv[:, c, 1], EPS, None, ALU.add).then_inc(var_ready, 1)

            def ln_factors(i, slot):
                c = slice(TPC * slot, TPC * (slot + 1))
                dve.wait_ge(std_ready, i + 1)
                own.add(dve.reciprocal(rstd[:, c], std[:, c]))
                own.wait()
                own.add(dve.tensor_tensor(newton[:, c], rstd[:, c], rstd[:, c], ALU.mult))
                own.wait()
                own.add(dve.tensor_tensor(newton[:, c], newton[:, c], vareps[:, c], ALU.mult))
                own.wait()
                own.add(dve.tensor_scalar(newton[:, c], newton[:, c], -0.5, 1.5, ALU.mult, ALU.add))
                own.wait()
                own.add(dve.tensor_tensor(rstd[:, c], rstd[:, c], newton[:, c], ALU.mult))
                own.wait()
                dve.scalar_tensor_tensor(out=nbias[:, c], in0=mv[:, c, 0], scalar=-1.0, in1=rstd[:, c],
                                         op0=ALU.mult, op1=ALU.mult).then_inc(ln_ready, 1)

            def transposed(i, total):
                dve.wait_ge(xt_high, total + i + 1)
                at = slice(2 * P * i, 2 * P * (i + 1))
                dve.tensor_tensor(XTl[:, :, at], PS[:, i % 2, :].rearrange("p (k t) -> p k t", k=KT),
                                  XTh[:, :, at].bitcast(F32), ALU.subtract).then_inc(xt_low, 1)

            def ln_stats_x(i):
                dve.wait_ge(x_in[i], 16)
                ln_stats(i, lambda t: X[:, TPC * i + t, :], i)

            ln_stats_x(0)
            for i in range(NX):
                if i + 1 < NX:
                    ln_stats_x(i + 1)
                ln_factors(i, i)
                if i >= 1:
                    transposed(2 * i - 2, 0)
                    transposed(2 * i - 1, 0)
            transposed(2 * NX - 2, 0)
            transposed(2 * NX - 1, 0)
            dve.wait_ge(kvw_ready, 1)
            for w in (1, 0):
                dve.tensor_tensor(Wl[:, w], Wr[:, w], Wh[:, w].bitcast(F32), ALU.subtract).then_inc(kvw_ready, 1)

            halves = [slice(0, CH), slice(CH, 2 * CH)]
            dve.wait_ge(cs_in, 16)

            def rope_products(i, half):
                def table(k):
                    return CS[:, k:k + 1, half].broadcast_to([P, 2, CH])

                dve.wait_ge(proj_done, i + 1)
                own.add(dve.tensor_tensor(tc[:], SD, table(0), ALU.mult))
                dve.tensor_tensor(ts[:], SD, table(1), ALU.mult).then_inc(proj_read, 1)

            def rope_parts(i, half, stage_waits=()):
                dve.wait_ge(proj_read, i + 1)
                own.wait()
                own.add(dve.tensor_tensor(EO[:, 0, :], tc[:, 0, :], ts[:, 1, :], ALU.subtract))
                own.add(dve.tensor_tensor(EO[:, 1, :], tc[:, 1, :], ts[:, 0, :], ALU.add))
                own.wait()
                for s, v in stage_waits:
                    dve.wait_ge(s, v)
                own.add(dve.tensor_copy(ST[:, 0:2, half], EO[:]))
                own.wait()
                dve.tensor_tensor(ST[:, 2:4, half], EO[:], ST[:, 0:2, half].bitcast(F32), ALU.subtract
                                  ).then_inc(rope_done, 1)

            def rope(i, half, stage_waits=()):
                rope_products(i, half)
                rope_parts(i, half, stage_waits)

            for i in range(NPROJ):
                rope(i, halves[i % 2], [(k_stored[i % 2], 16 * (i // 2))] if i >= 2 else [])
            for c in range(2):
                rope(NPROJ + c, halves[c], [(k_stored[c], 16 * NPROJ // 2)])
            dve.wait_ge(bo_in, 16)

            def normalise(n, p, c):
                m = 4 * n + 2 * p + c
                dve.wait_ge(pv_done, NU * n + PU * p + (3, PU)[c])
                pv = PV.rearrange("p h (t w) -> p h t w", w=VN)
                own.add(dve.reciprocal(RC[:].unsqueeze(3), pv[:, :, :, DH:DH + 1]))
                own.wait()
                if not isinstance(m, int) or m >= 2:
                    dve.wait_ge(ctxT_done, m - 1)
                dve.tensor_tensor(CTX[c][:].rearrange("p t h d -> p h t d"), pv[:, :, :, 0:DH],
                                  RC[:].unsqueeze(3).broadcast_to([P, 2, TPC, DH]), ALU.mult).then_inc(norm_done, 1)

            def split_context(m):
                dve.wait_ge(ctxT_done, m + 1)
                if not isinstance(m, int) or m >= 1:
                    dve.wait_ge(y_done, 2 * m)
                src = SD[:, 0, :].rearrange("p (t s) -> p t s", t=TPC)
                own.add(dve.tensor_copy(CTh[:], src))
                own.wait()
                dve.tensor_tensor(CTl[:], src, CTh[:].bitcast(F32), ALU.subtract).then_inc(split_done, 1)

            def add_out(m, b, c, half):
                dve.wait_ge(y_done, 2 * m + half + 1)
                t = NB // B * b + TPC * c + 2 * half
                acc = yacc[:, t:t + 2, :]
                dve.tensor_tensor(acc, SD[:, 1, :].rearrange("p (t d) -> p t d", t=2), acc, ALU.add).then_inc(y_added, 1)

            def body(g, first=False, last=False):
                for b in range(B):
                    n = 2 * g + b
                    more = not (last and b == B - 1)
                    for p in range(2):
                        m = 4 * n + 2 * p
                        if more and p == 1:
                            rope_parts(NPROJ + 2 * n + 3, halves[1])
                        if not (first and b == 0 and p == 0):
                            split_context(m - 1)
                            if p == 0:
                                add_out(m - 1, 1 - b, 1, 0)
                        normalise(n, p, 0)
                        if not (first and b == 0 and p == 0):
                            if p == 1:
                                add_out(m - 1, b, 1, 0)
                            add_out(m - 1, b if p == 1 else 1 - b, 1, 1)
                        if more and p == 0:
                            rope(NPROJ + 2 * n + 2, halves[0], [(qs_in[i], QT * (n + 1)) for i in range(2)])
                        split_context(m)
                        add_out(m, b, 0, 0)
                        if p == 0:
                            add_out(m, b, 0, 1)
                        normalise(n, p, 1)
                        if more and p == 0:
                            rope_products(NPROJ + 2 * n + 3, halves[1])
                        if p == 1:
                            add_out(m, b, 0, 1)

            steps = B * (2 * 4 + 2 * 4)
            body(0, first=True)
            begun = own.base + own.k
            with dve.Fori(1, G - 1) as g:
                own.base, own.k = begun + steps * (g - 1), 0
                body(g)
                assert own.k == steps
            own.base, own.k = begun + steps * (G - 2), 0
            body(G - 1, last=True)
            M = 4 * B * G
            split_context(M - 1)
            for half in range(2):
                add_out(M - 1, 1, 1, half)

            dve.wait_ge(y_added, 2 * M)

            def stats_of(k):
                i = k % NX
                if k < 2 * NX:
                    ln_stats(k, lambda t: yacc[:, TPC * i + t, :], i)
                    return
                if i == 0:
                    dve.wait_ge(x2_in, 16)
                dve.wait_ge(yn_ready, TPC * (i + 1))
                c = slice(TPC * i, TPC * (i + 1))
                own.add(dve.tensor_tensor(X2[:, c, :], X2[:, c, :], yacc[:, c, :], ALU.add))
                own.wait()
                ln_stats(k, lambda t: X2[:, TPC * i + t, :], i)

            stats_of(NX)
            for k in range(NX, 3 * NX):
                if k + 1 < 3 * NX:
                    stats_of(k + 1)
                ln_factors(k, k % NX)
                if k == NX:
                    dve.wait_ge(rw_ready, 1)
                    dve.tensor_tensor(Rl[:], Rr[:], Rh[:].bitcast(F32), ALU.subtract).then_inc(rw_ready, 1)
                if k > 2 * NX:
                    for i in range(2 * (k - 2 * NX) - 2, 2 * (k - 2 * NX)):
                        transposed(i, NB // 2)
            transposed(2 * NX - 2, NB // 2)
            transposed(2 * NX - 1, NB // 2)

            dve.wait_ge(lg_done, 1)
            own.add(dve.tensor_copy(LG[:], PS[:, 6, 0:16 * NB].rearrange("p (t r) -> p t r", r=16)[:, :, 0:NG]))
            own.wait()
            dve.tensor_scalar(ex[:, 1, :], LG[:, :, NE], -1.0, None, ALU.mult).then_inc(gap_ready, 1)
            for t in range(NB):
                own.add(dve.max(top[:, t, :], LG[:, t, 0:NE]))
            own.wait()
            dve.tensor_tensor(ex[:, 0, :], top[:, :, 1], top[:, :, 0], ALU.subtract).then_inc(gap_ready, 1)
            for t in range(NB):
                own.add(dve.max_index(topi[:, t, :], top[:, t, :], LG[:, t, 0:NE]))
            own.wait()
            own.add(dve.tensor_copy(topf[:], topi[:]))
            dve.wait_ge(e2_ready, 1)
            own.add(dve.tensor_scalar(den[:], ex[:], 1.0, None, ALU.add))
            own.wait()
            own.add(dve.reciprocal(wt[:, 0:2, :], den[:]))
            own.wait()
            own.add(dve.tensor_tensor(wt[:, 2, :], ex[:, 0, :], wt[:, 0, :], ALU.mult))
            own.wait()
            for e in range(NE):
                own.add(dve.scalar_tensor_tensor(out=CB[:, :, e], in0=topf[:, :, 0], scalar=float(e), in1=wt[:, 0, :],
                                                 op0=ALU.is_equal, op1=ALU.mult))
                own.add(dve.scalar_tensor_tensor(out=CB2[:, :, e], in0=topf[:, :, 1], scalar=float(e), in1=wt[:, 2, :],
                                                 op0=ALU.is_equal, op1=ALU.mult))
            own.wait()
            own.add(dve.tensor_tensor(CB[:, :, 0:NE], CB[:, :, 0:NE], CB2[:, :, 0:NE], ALU.add))
            own.add(dve.tensor_copy(CB[:, :, NE], wt[:, 1, :]))
            own.wait()
            own.add(dve.tensor_copy(CBh[:], CB[:]))
            own.wait()
            dve.tensor_copy(CBx[:, :, 0:NG], CBh[:].bitcast(F32)).then_inc(cb_ready, 1)
            dve.tensor_tensor(CBx[:, :, NG:2 * NG], CB[:], CBh[:].bitcast(F32), ALU.subtract).then_inc(cb_ready, 1)
            dve.wait_ge(ct_zero, 1)
            for i in range(NB // 4):
                dve.wait_ge(cbT_done, i + 1)
                dve.tensor_copy(CT[0:2 * NG, CH * i:CH * (i + 1)], PS[0:2 * NG, 2 + i, :]).then_inc(cbT_read, 1)

            def chunk(q, first=False):
                for j in range(NT):
                    n = NT * q + j
                    bank = 3 * (j % 2)
                    dve.wait_ge(silu_done, n + 1)
                    if not first or j >= 2:
                        dve.wait_ge(hh_done, n - (j > 0))
                        dve.wait_ge(hl_done, n - (j > 0))
                    own.add(dve.tensor_tensor(hd[:, j % 2, :], PS[:, bank + 1, :], sg[:, j % 2, :], ALU.mult))
                    own.wait()
                    dve.tensor_tensor(hd[:, j % 2, :], PS[:, bank + 2, :], hd[:, j % 2, :], ALU.mult).then_inc(hid_done, 1)
                    if not first and j == 1:
                        dve.wait_ge(fy_read, q)
                        ln_stats(3 * NX + q - 1, lambda t: Y[:, t, :], 0)
                    if not first and j == 3:
                        ln_factors(3 * NX + q - 1, 0)
                    if not first and j == 5:
                        residual(q - 1)
                    dve.wait_ge(hh_done, n + 1)
                    if not first or j >= NH:
                        dve.wait_ge(down_done, n - (1 if j < 2 else 2))
                    dve.tensor_tensor(Hl[:, j % NH, :], hd[:, j % 2, :], Hh[:, j % NH, :].bitcast(F32), ALU.subtract
                                      ).then_inc(hl_done, 1)

            def residual(q):
                dve.wait_ge(fn_ready, TPC * q + TPC)
                dve.tensor_tensor(O, O, X2[:, bass.ds(TPC * q, TPC), :], ALU.add).then_inc(o_ready, 1)

            steps = NT + 2 * TPC + 5
            chunk(0, first=True)
            begun = own.base + own.k
            with dve.Fori(1, NX) as q:
                own.base, own.k = begun + steps * (q - 1), 0
                chunk(q)
                assert own.k == steps, own.k
            own.base, own.k = begun + steps * (NX - 1), 0
            dve.wait_ge(fy_read, NX)
            ln_stats(4 * NX - 1, lambda t: Y[:, t, :], 0)
            ln_factors(4 * NX - 1, 0)
            residual(NX - 1)




def _tables():
    inv = (1.0 / 10000.0 ** (np.arange(0, DH, 2, dtype=np.float32) / DH)).astype(np.float32)
    angle = np.arange(S, dtype=np.float32)[None, :] * inv[:, None]
    cs = np.stack([np.tile(np.cos(angle), (4, 1)), np.tile(np.sin(angle), (4, 1))], 1).astype(np.float32)

    def part(v):
        m, e = np.frexp(v)
        return np.ldexp(np.round(m * 4096) / 4096, e)

    pos = np.arange(S, dtype=np.float64)
    al = np.zeros((G * 4 + R * 4, S))
    for g in range(G):
        al[4 * g:4 * g + 2] = pos * 2.0 ** -g
        al[4 * g + 2:4 * g + 4] = 2.0 ** -g
    for h in range(R):
        slope = 2.0 ** (-(h + 1) * 8.0 / H)
        rows = []
        for v in (np.full(S, slope), -slope * pos):
            rows += [part(v), part(v - part(v))]
        al[4 * G + 4 * h:4 * G + 4 * h + 4] = rows
    sel = np.zeros((2 * NG, NT * P), np.float32)
    for i in range(HID):
        e = min(i // IM, NE)
        sel[e, i] = sel[NG + e, i] = 1.0
    return cs, al.astype(np.float32), np.eye(P, dtype=np.float32), sel


def kernel(**inputs):
    import concourse.bacc as _bacc
    from concourse.bass_utils import run_bass_kernel_spmd as _run

    a = {k[3:]: np.asarray(v) for k, v in inputs.items()}
    cs, al, ident, sel = _tables()
    x = a["attn_hidden_states"].reshape(TOK, D)
    wq = a["attn_Wq"].reshape(KT, P, G, R, 32, 2).transpose(2, 1, 0, 5, 3, 4).reshape(G, P, KT, 2, P)
    wk = a["attn_Wk"].reshape(KT, P, 2, 4, 32, 2).transpose(1, 0, 2, 5, 3, 4).reshape(P, KT, CH)
    wv = a["attn_Wv"].reshape(KT, P, CH).transpose(1, 0, 2)
    wo = a["attn_Wo"].reshape(G, 2, P, D).transpose(0, 2, 1, 3)
    gu, dn = a["ffn_gate_up_proj"], a["ffn_down_proj"]
    pad = np.zeros((NT * P - HID, D), np.float32)
    gate = np.concatenate([gu[:, :IM].reshape(NE * IM, D), a["ffn_sh_gate_w"], pad])
    up = np.concatenate([gu[:, IM:].reshape(NE * IM, D), a["ffn_sh_up_w"], pad])
    down = np.concatenate([dn.transpose(0, 2, 1).reshape(NE * IM, D), a["ffn_sh_down_w"].T, pad])
    tiles = [w.reshape(NT, P, KT, P).transpose(0, 3, 2, 1).reshape(NT, P, D) for w in (gate, up)]
    wf = np.concatenate([*tiles, down.reshape(NT, P, D)], axis=2)
    wr = np.concatenate([a["ffn_router_weight"], a["ffn_shared_gate_w"], np.zeros((P - NG, D), np.float32)])
    wr = wr.reshape(P, KT, P).transpose(2, 1, 0)

    nc = _bacc.Bacc("TRN2", target_bir_lowering=False, num_devices=1)
    arrays, args = {}, []
    for name, v in dict(x=x, wq=wq, wk=wk, wv=wv, wo=wo, bo=a["attn_bo"], wf=wf, wr=wr, cs=cs, al=al,
                        ident=ident, sel=sel).items():
        v = np.ascontiguousarray(v)
        arrays[f"in_{name}"] = v
        args.append(nc.dram_tensor(f"in_{name}", v.shape, mybir.dt.from_np(v.dtype), kind="ExternalInput").ap())
    args.append(nc.dram_tensor("out_0", (TOK, D), F32, kind="ExternalOutput").ap())
    build(nc, *args)
    r = _run(nc, [arrays], core_ids=[0])
    return r.results[0]["out_0"].reshape(B, S, D)
```

```python
from contextlib import ExitStack

import numpy as np
import concourse.bass as bass
from concourse import mybir

F32 = mybir.dt.float32
F32R = mybir.dt.float32r
U32 = mybir.dt.uint32
ALU = mybir.AluOpType
ACT = mybir.ActivationFunctionType

P = 128
B, S, D = 2, 1024, 256
TOK = B * S
NB = TOK // P
H, G, DH = 32, 8, 64
R = H // G
KT = D // P
CH = 512
NE, IM, ISH = 8, 176, 704
HID = NE * IM + ISH
NT = -(-HID // P)
SHARED = -(-NE * IM // P)
TAIL = HID - (NT - 1) * P
assert TAIL == P // 2
NG = NE + 1
NH = 3
EPS = 1e-5
CAP = 30.0
TPC = CH // P
HB = NB // B



def unit_pieces(u):
    def diagonal(hh, c):
        return [(hh, 4 * c, CH * c, CH, 0), (hh, 4 * c + 3, CH * c + 384, 128, CH),
                (hh, 4 * c + 1, CH * c + 128, 384, CH + 128)]

    def rest(c):
        return [(hh, 4 * c + 2, CH * c + 256, 256, 256 * hh) for hh in range(2)]

    def full(hh, t):
        return [(hh, t, CH, CH, 0), (hh, t + 1, CH, CH, CH)]

    return [diagonal(0, 0), diagonal(1, 0), rest(0), full(0, 0), full(0, 2), diagonal(0, 1),
            full(1, 0), full(1, 2), diagonal(1, 1), rest(1)][u]


AHEAD = 4
NP = 4
PU = 10
NU = 2 * PU
WIDTH = [sum(p[3] for p in unit_pieces(u)) for u in range(PU)]
MASKED = [u for u in range(PU) if u not in (3, 4, 6, 7)]
NM = 2 * len(MASKED)
CHUNK_END = {2: 0, 9: 1}
CHUNK_START = {0: 0, 3: 1}


def masked_count(n, u):
    p, v = divmod(u, PU)
    return NM * n + len(MASKED) * p + MASKED.index(v) + 1


def wait_apart(eng, sem, value, passed):
    eng.wait_ge(sem, value)
    if not isinstance(value, int):
        eng.sem_inc(passed, 1)


class Steps:

    def __init__(self, eng, sem):
        self.eng, self.sem, self.base, self.k = eng, sem, 0, 0

    def add(self, instruction):
        instruction.then_inc(self.sem, 1)
        self.k += 1
        return self.k

    def wait(self, k=None):
        self.eng.wait_ge(self.sem, self.base + (self.k if k is None else k))

    def wait_apart(self, passed):
        wait_apart(self.eng, self.sem, self.base + self.k, passed)


def build(nc, x, wq, wk, wv, wo, bo, wf, wr, cs, al, ident, sel, out):
    with ExitStack() as ctx:
        def sem(name):
            return ctx.enter_context(nc.semaphore(name))

        def sb(stack, name, shape, dt=F32):
            return stack.enter_context(nc.sbuf_tensor(name, shape, dt))

        ks_dram = nc.dram_tensor("ks_scratch", (4, G * 32, TOK), F32, kind="Internal").ap()
        ka_dram = nc.dram_tensor("ka_scratch", (G * 4, S), F32, kind="Internal").ap()

        PS = ctx.enter_context(nc.psum_tensor("PS", [P, 8, CH], F32))
        SC = PS[:, 0:4, :].rearrange("p (b k) n -> p b (k n)", b=2)
        PV = PS[:, 4:6, :]
        SD = PS[:, 6:8, :]

        XTh = sb(ctx, "XTh", [P, KT, TOK], F32R)
        XTl = sb(ctx, "XTl", [P, KT, TOK], F32R)
        yacc = sb(ctx, "yacc", [P, NB, D])
        idn = sb(ctx, "idn", [P, P])
        stats = sb(ctx, "stats", [P, NB, 6])
        mv = sb(ctx, "mv", [P, NB, 2])
        vareps = sb(ctx, "vareps", [P, NB])
        std = sb(ctx, "std", [P, NB])
        rstd = sb(ctx, "rstd", [P, NB])
        newton = sb(ctx, "newton", [P, NB])
        nbias = sb(ctx, "nbias", [P, NB])

        att = ExitStack()
        KKa, KKb = [], []
        for b in range(B):
            if b == B - 1:
                with ExitStack() as early:
                    KS0 = sb(early, "KS0", [P, 4, CH], F32R)
            KKa.append(sb(att, f"KKa{b}", [P, S], F32R))
            KKb.append(sb(att, f"KKb{b}", [P, S], F32R))
        ST = sb(att, "ST", [P, 4, S], F32R)
        EO = [sb(att, "EO0", [P, 2, CH])]
        ts = sb(att, "ts", [P, 2, CH])
        CS = sb(att, "CS", [P, 2, S])
        V = sb(att, "V", [P, NB, G, DH])
        EO.append(sb(att, "EO1", [P, 2, CH]))
        RS, CX = EO[1][:, 0, :], EO[1][:, 1, :]
        WQr = sb(att, "WQr", [P, KT, 2, P])
        WQh = sb(att, "WQh", [P, KT, 2, P], F32R)
        WQl = sb(att, "WQl", [P, KT, 2, P], F32R)
        WOr = sb(att, "WOr", [P, 2, D])
        WOh = sb(att, "WOh", [P, 2, D], F32R)
        WOl = sb(att, "WOl", [P, 2, D], F32R)
        VS = [sb(att, "VS0", [P, S + DH])]
        with ExitStack() as early:
            KS1 = sb(early, "KS1", [P, 4, CH], F32R)
        VS.append(sb(att, "VS1", [P, S + DH]))
        CTh = sb(att, "CTh", [P, TPC, P], F32R)
        CTl = sb(att, "CTl", [P, TPC, P], F32R)
        pro = ExitStack()
        X = sb(pro, "X", [P, NB, D])
        Wr = sb(pro, "Wr", [P, 2, KT, CH])
        ALr = sb(pro, "ALr", [48, S])
        ALh = sb(pro, "ALh", [48, S], F32R)
        Wh = sb(pro, "Wh", [P, 2, KT, CH], F32R)
        Wl = sb(pro, "Wl", [P, 2, KT, CH], F32R)
        pro.close()
        QSa = sb(att, "QSa", [P, R, S], F32R)
        QSb = sb(att, "QSb", [P, R, S], F32R)
        PR = sb(att, "PR", [P, NP, 2 * CH])
        att.close()

        ffn = ExitStack()
        X2 = sb(ffn, "X2", [P, NB, D])
        SL = sb(ffn, "SL", [P, NT * P], F32R)
        with ExitStack() as early:
            SLr = sb(early, "SLr", [P, NT * P])
        CT = sb(ffn, "CT", [P, TOK], F32R)
        LG = sb(ffn, "LG", [P, HB, NG])
        top = sb(ffn, "top", [P, HB, 8])
        Rr = sb(ffn, "Rr", [P, KT, P])
        Rh = sb(ffn, "Rh", [P, KT, P], F32R)
        Rl = sb(ffn, "Rl", [P, KT, P], F32R)
        topi = sb(ffn, "topi", [P, HB, 8], U32)
        topf = sb(ffn, "topf", [P, HB, 8])
        ex = sb(ffn, "ex", [P, 2, HB])
        den = sb(ffn, "den", [P, 2, HB])
        wt = sb(ffn, "wt", [P, 3, HB])
        CB = sb(ffn, "CB", [P, HB, NG])
        CB2 = sb(ffn, "CB2", [P, HB, NG])
        CBh = sb(ffn, "CBh", [P, HB, NG], F32R)
        CBx = sb(ffn, "CBx", [P, HB, 2 * NG])
        WFr = sb(ffn, "WFr", [P, 2, 3 * D])
        WF = sb(ffn, "WF", [P, NT, 2, 3 * D], F32R)
        WFh, WFl = WF[:, :, 0, :], WF[:, :, 1, :]
        Hh = sb(ffn, "Hh", [P, NH, CH], F32R)
        Hl = sb(ffn, "Hl", [P, NH, CH], F32R)
        ffn.close()
        sg, hd, Y, O = (yacc[:, 4 * i:4 * i + 4, :].rearrange("p (a b) d -> p a (b d)", a=2) for i in range(4))
        Y, O = (t.rearrange("p a (b d) -> p (a b) d", b=2) for t in (Y, O))
        LT = [yacc[0:NG, HB * b + HB // 2:HB * (b + 1), :].rearrange("p t d -> p (t d)") for b in range(B)]

        FY = PS[:, 6:8, :].rearrange("p b (t d) -> p (b t) d", t=2)

        NX = NB // TPC
        x_in = [sem(f"x_in{i}") for i in range(NX)]
        kv_in = [sem("wk_in"), sem("wv_in")]
        cs_in, id_in, al_in, bo_in, q_in, o_in = (sem(n) for n in
            ("cs_in", "id_in", "al_in", "bo_in", "q_in", "o_in"))
        dve_step, pool_step = sem("dve_step"), sem("pool_step")
        dve_passed, pool_passed = sem("dve_passed"), sem("pool_passed")
        var_ready, std_ready, ln_ready, xn_ready, fn_ready = (sem(n) for n in
            ("var_ready", "std_ready", "ln_ready", "xn_ready", "fn_ready"))
        xt_psum, xt_high, xt_low = sem("xt_psum"), sem("xt_high"), sem("xt_low")
        high_ready = [sem("k_high_ready"), sem("v_high_ready")]
        low_ready = [sem("k_low_ready"), sem("v_low_ready")]
        v_psum, v_ready, v_ones = sem("v_psum"), sem("v_ready"), [sem(f"v_ones{b}") for b in range(B)]
        vs_in = [sem(f"vs_in{b}") for b in range(B)]
        al_ready, ka_stored, slope_rows = sem("al_ready"), sem("ka_stored"), sem("slope_rows")
        k_stored = [sem(f"k_stored{i}") for i in range(2)]
        ks1_stored, last_k_stored = sem("ks1_stored"), sem("last_k_stored")
        kk_in = [sem(f"kk_in{b}") for b in range(B)]
        qs_in = [sem(f"qs_in{p}") for p in range(2)]
        proj_done, proj_read, rope_done = sem("proj_done"), sem("proj_read"), sem("rope_done")
        eo_ready, rope_high = sem("eo_ready"), sem("rope_high")
        wq_ready, wo_ready = sem("wq_ready"), sem("wo_ready")
        qk_done, tanh_done, exp_done, mask_done, pv_done = (sem(n) for n in
            ("qk_done", "tanh_done", "exp_done", "mask_done", "pv_done"))
        sums_read, ctx_read, split_done, y_done, y_added = (sem(n) for n in
            ("sums_read", "ctx_read", "split_done", "y_done", "y_added"))
        x2_in = [sem(f"x2_in{b}") for b in range(B)]
        r_in, rw_ready, lt_done, lt_read, lg_done, cb_ready, cbT_done, cbT_read, ct_zero = (sem(n) for n in
            ("r_in", "rw_ready", "lt_done", "lt_read", "lg_done", "cb_ready", "cbT_done", "cbT_read", "ct_zero"))
        lg_read, gap_ready, e2_ready, sel_zero, sel_in, sel_ready = (sem(n) for n in
            ("lg_read", "gap_ready", "e2_ready", "sel_zero", "sel_in", "sel_ready"))
        wf_in = [sem(f"wf_in{i}") for i in range(2)]
        wfh_ready, wfl_ready = sem("wfh_ready"), sem("wfl_ready")
        guc_done, silu_done, hid_done, hh_done, hl_done, down_done = (sem(n) for n in
            ("guc_done", "silu_done", "hid_done", "hh_done", "hl_done", "down_done"))
        fy_read, o_ready, o_out = (sem(n) for n in ("fy_read", "o_ready", "o_out"))

        NPROJ = 8
        PROJECTIONS = [(0, 0), (0, 1), (0, 2), (0, 3), (None, 0), (None, 1), (1, 0), (1, 1), (1, 2), (1, 3)]
        NPRE = len(PROJECTIONS)
        VALUES_AFTER = {4: (8, 9), 5: (10, 11), 6: (12, 13), 7: (14,), 8: (15,), 9: ()}

        SPARE_FROM = 7
        FIRST_GATE_BANK = [2 if j >= SPARE_FROM else 3 * (j % 2) + 2 for j in range(NT)]
        GATE_BANK = [3 * (min(j, SHARED) % 2) + 2 for j in range(NT)]

        def units(j):
            return slice(0, TAIL if j == NT - 1 else P)

        def side_banks(i):
            return PV if isinstance(i, int) and i < NPRE and i % 2 else SD

        def rotated_in(i):
            return i % 2 if isinstance(i, int) and i < NPRE else 0

        def staging(i):
            half = slice(CH * (i % 2), CH * (i % 2 + 1))
            return KS0[:] if i == 6 else KS1[:] if i == 7 else ST[:, :, half]

        QT = 16 * 12
        M = 4 * B * G
        KL = 16 * 7

        block = ctx.enter_context(nc.Block())

        @block.sync
        def _(sp):
            xv = x.rearrange("(q t p) d -> q p t d", p=P, t=TPC)
            for i in range(NX):
                sp.dma_start(X[:, TPC * i:TPC * (i + 1), :], xv[i]).then_inc(x_in[i], 16)
                if i == 0:
                    sp.dma_start(idn[:], ident).then_inc(id_in, 16)
                    sp.dma_start(Wr[:, 0], wk).then_inc(kv_in[0], 16)
                if i == 1:
                    sp.dma_start(Wr[:, 1], wv).then_inc(kv_in[1], 16)
            sp.dma_start(CS[:], cs).then_inc(cs_in, 16)
            sp.dma_start(WQr[:], wq[0]).then_inc(q_in, 16)
            sp.dma_start(ALr[:], al).then_inc(al_in, 16)
            sp.dma_start(WOr[:], wo[0]).then_inc(o_in, 16)
            sp.dma_start(yacc[:], bo.partition_broadcast(P).unsqueeze(1).broadcast_to([P, NB, D])
                         ).then_inc(bo_in, 16)

            def store_keys(i):
                s, q = PROJECTIONS[i]
                sp.wait_ge(rope_done, i + 1)
                sp.dma_start(ks_dram[:, P * s:P * (s + 1), CH * q:CH * (q + 1)].rearrange("k p n -> p k n"),
                             staging(i).bitcast(F32)
                             ).then_inc(k_stored[i % 2] if i < 4 else ks1_stored if i == 7 else last_k_stored, 16)

            def load_keys(g, b):
                for quarter in range(4):
                    sp.dma_start(KKa[b][32 * quarter:32 * quarter + 32, :].bitcast(F32),
                                 ks_dram[quarter % 2, bass.ds(32 * g, 32), S * b:S * (b + 1)]).then_inc(kk_in[b], 16)
                for quarter in range(2):
                    sp.dma_start(KKb[b][32 * quarter:32 * quarter + 32, :].bitcast(F32),
                                 ks_dram[2 + quarter, bass.ds(32 * g, 32), S * b:S * (b + 1)]).then_inc(kk_in[b], 16)
                sp.dma_start(KKb[b][64:68, :].bitcast(F32), ka_dram[bass.ds(4 * g, 4), :]).then_inc(kk_in[b], 16)

            def load_values(g, b):
                sp.dma_start(VS[b][:, DH:DH + S].rearrange("p (t w) -> p t w", w=2 * DH)[:, :, 0:DH],
                             V[:, HB * b:HB * (b + 1), bass.ds(g, 1), :].squeeze(2)).then_inc(vs_in[b], 16)

            def move_queries(p):
                for h in (2 * p, 2 * p + 1):
                    for kind in range(4):
                        sp.dma_start(QSa[32 * kind:32 * kind + 32, h, :].bitcast(F32),
                                     ST[32 * h:32 * h + 32, kind, :].bitcast(F32)).then_inc(qs_in[p], 16)
                    for kind in range(2):
                        sp.dma_start(QSb[32 * kind:32 * kind + 32, h, :].bitcast(F32),
                                     ST[32 * h:32 * h + 32, kind, :].bitcast(F32)).then_inc(qs_in[p], 16)

            for i in range(4):
                store_keys(i)
            sp.wait_ge(al_ready, 1)
            sp.dma_start(ka_dram, ALh[0:32, :].bitcast(F32)).then_inc(ka_stored, 16)
            for w in range(2):
                sp.wait_ge(low_ready[w], 1)
            for h in range(R):
                sp.dma_start(QSb[64:68, h, :].bitcast(F32), ALh[32 + 4 * h:36 + 4 * h, :].bitcast(F32)).then_inc(slope_rows, 16)
            for i in range(2):
                sp.wait_ge(k_stored[i], 16 * 2)
            sp.wait_ge(ka_stored, 16)
            sp.wait_ge(slope_rows, 16 * R)
            load_keys(0, 0)
            sp.wait_ge(v_ready, HB)
            sp.wait_ge(v_ones[0], 1)
            load_values(0, 0)
            sp.wait_ge(rope_done, 6)
            sp.wait_ge(xt_psum, NB // 2)
            move_queries(0)
            move_queries(1)
            for i in range(6, NPRE):
                store_keys(i)
            sp.wait_ge(ks1_stored, 16)
            sp.wait_ge(last_k_stored, 16 * 3)
            load_keys(0, 1)
            sp.wait_ge(v_ready, NB)
            sp.wait_ge(v_ones[1], 1)
            load_values(0, 1)

            def body(g, last=False):
                for b in range(B):
                    n = 2 * g + b
                    if not last:
                        if b == 0:
                            sp.wait_ge(wq_ready, g + 1)
                            sp.dma_start(WQr[:], wq[bass.ds(g + 1, 1)].squeeze(0)).then_inc(q_in, 16)
                        else:
                            sp.wait_ge(wo_ready, g + 1)
                            sp.dma_start(WOr[:], wo[bass.ds(g + 1, 1)].squeeze(0)).then_inc(o_in, 16)
                    if not (last and b == B - 1):
                        sp.wait_ge(rope_done, NPROJ + 2 * n + 4)
                        sp.wait_ge(qk_done, NU * n + PU)
                        move_queries(0)
                        sp.wait_ge(qk_done, NU * n + NU)
                        move_queries(1)
                        if not last:
                            load_keys(g + 1, b)
                            sp.wait_ge(pv_done, NU * n + NU)
                            load_values(g + 1, b)

            body(0)
            with sp.Fori(1, G - 1) as g:
                body(g)
            body(G - 1, last=True)

            xb = x.rearrange("(b t p) d -> b p t d", p=P, b=B)
            sp.dma_start(X2[:, 0:HB, :], xb[0]).then_inc(x2_in[0], 16)
            for p in range(2):
                sp.wait_ge(qs_in[p], QT * B * G)
            sp.dma_start(Rr[:], wr).then_inc(r_in, 16)
            sp.dma_start(SLr[0:2 * NG, :], sel).then_inc(sel_in, 16)
            for j in range(NT):
                if j == 2:
                    sp.wait_ge(qk_done, NU * B * G)
                    sp.dma_start(X2[:, HB:NB, :], xb[1]).then_inc(x2_in[1], 16)
                if j >= 2:
                    sp.wait_ge(wfl_ready, j - 1)
                sp.dma_start(WFr[:, j % 2], wf[j]).then_inc(wf_in[j % 2], 16)
            ov = out.rearrange("(q t p) d -> q p t d", p=P, t=TPC)
            with sp.Fori(0, NX) as q:
                for h in range(2):
                    sp.wait_ge(o_ready, 2 * q + h + 1)
                    half = slice(TPC // 2 * h, TPC // 2 * (h + 1))
                    sp.dma_start(ov[bass.ds(q, 1)].squeeze(0)[:, half, :], O[:, half, :]).then_inc(o_out, 16)
            sp.wait_ge(o_out, 32 * NX)

        @block.tensor
        def _(pe):
            def three(dst, ah, al_, bh, bl, kts, first=True, last=True, **kw):
                terms = [(a(k), b(k)) for k in kts for a, b in ((ah, bh), (ah, bl), (al_, bh))]
                for i, (a, b) in enumerate(terms):
                    mm = pe.matmul(dst, a, b, start=first and i == 0, stop=last and i == len(terms) - 1, **kw)
                return mm

            pe.wait_ge(id_in, 16)

            def transpose_x(i, src, t0, bank, reuse):
                pe.wait_ge(xn_ready, 2 * i + 2)
                if reuse > 0:
                    pe.wait_ge(xt_high, reuse)
                    pe.wait_ge(xt_low, reuse)
                dst = bank.rearrange("p (k t) -> p k t", k=KT)
                for t in range(2):
                    for k in range(KT):
                        mm = pe.transpose(dst[:, k, P * t:P * (t + 1)], src[:, t0 + t, P * k:P * (k + 1)], idn[:])
                mm.then_inc(xt_psum, 1)

            def transpose_new_x(b, i, bank, reuse):
                transpose_x(NB // 2 + HB // 2 * b + i, yacc, HB * b + 2 * i, bank, reuse)

            def router(b, c, bank):
                pe.wait_ge(rw_ready, 1)
                split = NB // 2 + HB // 2 * (b + 1)
                pe.wait_ge(xt_high, split)
                pe.wait_ge(xt_low, split)
                tok = slice(S * b + CH * c, S * b + CH * (c + 1))
                three(bank, lambda k: Rh[:, k, :], lambda k: Rl[:, k, :],
                      lambda k: XTh[:, k, tok], lambda k: XTl[:, k, tok], range(KT)).then_inc(lt_done, 1)

            def router_by_tokens(b, bank):
                pe.wait_ge(lt_read, 2 * b + 2)
                for t in range(HB):
                    mm = pe.transpose(bank[:, 16 * t:16 * t + NG], LT[b][:, P * t:P * (t + 1)], idn[0:NG, 0:NG])
                mm.then_inc(lg_done, 1)

            def transpose_gates(b, c, bank):
                pe.wait_ge(cb_ready, 2 * b + 2)
                for t in range(TPC):
                    mm = pe.transpose(bank[0:2 * NG, P * t:P * (t + 1)], CBx[:, TPC * c + t, :], idn[:])
                mm.then_inc(cbT_done, 1)

            def project(w_hi, w_lo, tokens, i):
                if not isinstance(i, int) or i >= NPRE:
                    pe.wait_ge(proj_read, i)
                elif i >= 2:
                    pe.wait_ge(proj_read, i - 1)
                for eo in range(2):
                    mm = three(side_banks(i)[:, eo, :], lambda k: w_hi(k, eo), lambda k: w_lo(k, eo),
                               lambda k: XTh[:, k, tokens], lambda k: XTl[:, k, tokens], range(KT))
                mm.then_inc(proj_done, 1)

            def values(t):
                if t >= 2:
                    pe.wait_ge(v_ready, t - 1)
                tok = slice(P * t, P * (t + 1))
                three(PS[:, 2 + t % 2, :], lambda k: XTh[:, k, tok], lambda k: XTl[:, k, tok],
                      lambda k: Wh[:, 1, k, :], lambda k: Wl[:, 1, k, :], range(KT)).then_inc(v_psum, 1)

            def queries(n, b, c):
                project(lambda k, eo: WQh[:, k, eo, :], lambda k, eo: WQl[:, k, eo, :],
                        slice(S * b + CH * c, S * b + CH * (c + 1)), NPROJ + 2 * n + c)

            def prologue_projection(i):
                s, q = PROJECTIONS[i]
                if s is None:
                    pe.wait_ge(wq_ready, 1)
                    w = [lambda k, eo: WQh[:, k, eo, :], lambda k, eo: WQl[:, k, eo, :]]
                else:
                    w = [lambda k, eo: Wh[:, 0, k, 256 * s + P * eo:256 * s + P * (eo + 1)],
                         lambda k, eo: Wl[:, 0, k, 256 * s + P * eo:256 * s + P * (eo + 1)]]
                project(*w, slice(CH * q, CH * (q + 1)), i)

            def turned_x(q):
                for i in range(2):
                    transpose_x(2 * q + i, X, TPC * q + 2 * i, PS[:, i, :], 2 * q + i - 1)

            turned_x(0)
            pe.wait_ge(low_ready[0], 1)
            for i in range(4):
                pe.wait_ge(xt_low, 2 * i + 2)
                prologue_projection(i)
                if i < 3:
                    turned_x(i + 1)
                if i == 0:
                    pe.wait_ge(low_ready[1], 1)
                values(2 * i)
                values(2 * i + 1)
            for i in range(4, NPRE):
                prologue_projection(i)
                for t in VALUES_AFTER[i]:
                    values(t)
            pe.wait_ge(v_ready, NB)
            pe.wait_ge(slope_rows, 16 * R)

            def scores(n, g, b, u):
                p, v = divmod(u, PU)
                if u == 0:
                    pe.wait_ge(kk_in[b], KL * (g + 1))
                if v == 0:
                    pe.wait_ge(qs_in[p], QT * (n + 1))
                U = NU * n + u
                if not isinstance(U, int) or U >= 2:
                    pe.wait_ge(tanh_done, U - 1)
                for hh, t, s0, w, col in unit_pieces(v):
                    dst = SC[:, u % 2, col:col + w]
                    keys, q = slice(P * t, P * (t + 1)), slice(s0, s0 + w)
                    pe.matmul(dst, KKa[b][:, keys], QSa[:, 2 * p + hh, q], start=True, stop=False)
                    mm = pe.matmul(dst, KKb[b][0:68, keys], QSb[0:68, 2 * p + hh, q], start=False, stop=True)
                mm.then_inc(qk_done, 1)

            def context(n, g, b, u):
                p, v = divmod(u, PU)
                if u == 0:
                    pe.wait_ge(vs_in[b], 16 * (g + 1))
                if v in MASKED:
                    pe.wait_ge(mask_done, masked_count(n, u))
                else:
                    pe.wait_ge(exp_done, NU * n + u + 1)
                if v in CHUNK_START:
                    m = 4 * n + 2 * p + CHUNK_START[v]
                    if not isinstance(m, int) or m >= 1:
                        pe.wait_ge(sums_read, m)
                        pe.wait_ge(ctx_read, m)
                started = {0: v not in (0, 3), 1: v not in (1, 6)}
                pieces = unit_pieces(v)
                for hh, t, s0, w, col in pieces:
                    at = 2 * DH * t + DH * (1 - hh)
                    mm = pe.matmul(PV[:, hh, s0 % CH:s0 % CH + w], VS[b][:, at:at + P], PR[:, u % NP, col:col + w],
                                   start=not started[hh], stop=v in CHUNK_END, skip_group_check=True)
                    started[hh] = True
                mm.then_inc(pv_done, 1)

            def project_out(m, p, projections, halves=(0, 1)):
                pe.wait_ge(split_done, m + 1)
                pe.wait_ge(proj_read, projections)
                if not isinstance(m, int) or m >= 1:
                    pe.wait_ge(y_added, m)
                for half in halves:
                    if halves[0] == 1 and half == 0:
                        pe.wait_ge(lg_read, 1)
                    for k in (2 * half, 2 * half + 1):
                        mm = three(SD[:, half, D * (k % 2):D * (k % 2 + 1)], lambda _: CTh[:, k, :],
                                   lambda _: CTl[:, k, :], lambda _: WOh[:, p, :], lambda _: WOl[:, p, :], [0])
                mm.then_inc(y_done, 1)

            def side(n, g, b, u, first, last):
                p, v = divmod(u, PU)
                m = 4 * n + 2 * p
                before = not (first and b == 0 and p == 0)
                more = not (last and b == B - 1)
                hoisted = not more and p == 1
                if more and p == 0 and v in (3, 5):
                    if b == B - 1 and v == 3:
                        pe.wait_ge(wq_ready, g + 2)
                    if before:
                        pe.wait_ge(y_added, m)
                    queries(n + 1, (b + 1) % B, v // 5)
                projections = NPROJ + 2 * n + 2
                if more:
                    projections += 2 if p == 1 or v > 5 else 0
                if v == 2 and before:
                    project_out(m - 1, 1 - p, projections)
                if hoisted:
                    if v in (5, 6):
                        i = 2 * v - 10
                        pe.wait_ge(y_added, m)
                        transpose_new_x(0, i, SD[:, 0, :], NB // 2 + i - 1)
                        transpose_new_x(0, i + 1, SD[:, 1, :], NB // 2 + i)
                    if v in (7, 8):
                        router(0, v - 7, SD[:, 8 - v, :])
                    if v == 9:
                        router_by_tokens(0, SD[:, 0, :])
                if v == 9:
                    if b == 0 and p == 0:
                        pe.wait_ge(wo_ready, g + 1)
                    project_out(m, p, projections, (1, 0) if hoisted else (0, 1))

            def body(g, first=False, last=False):
                for b in range(B):
                    n = 2 * g + b
                    for u in range(NU):
                        if u + AHEAD < NU:
                            scores(n, g, b, u + AHEAD)
                        elif b == 0:
                            scores(n + 1, g, 1, u + AHEAD - NU)
                        elif not last:
                            scores(n + 1, g + 1, 0, u + AHEAD - NU)
                        context(n, g, b, u)
                        side(n, g, b, u, first, last)

            for u in range(AHEAD):
                scores(0, 0, 0, u)
            pe.wait_ge(proj_read, NPRE)
            body(0, first=True)
            with pe.Fori(1, G - 1) as g:
                body(g)
            body(G - 1, last=True)

            def gate_up(q, j):
                if not isinstance(q, int) or q >= 1:
                    pe.wait_ge(hid_done, NT * q + j - (j > 0))
                elif j >= 2:
                    pe.wait_ge(hid_done, j - 1)
                tok = bass.ds(CH * q, CH)
                for part in range(1 if j == NT - 1 else 2):
                    mm = three(PS[:, 3 * (j % 2) + part, :], lambda k: WFh[:, j, 256 * part + P * k:256 * part + P * (k + 1)],
                               lambda k: WFl[:, j, 256 * part + P * k:256 * part + P * (k + 1)],
                               lambda k: XTh[:, k, tok], lambda k: XTl[:, k, tok], range(KT))
                if j > SHARED:
                    mm.then_inc(guc_done, 1)

            def gates(q, j, bank):
                if j > SHARED:
                    return
                pe.matmul(PS[:, bank, :], SL[:, P * j:P * (j + 1)], CT[:, bass.ds(CH * q, CH)], start=True, stop=True
                          ).then_inc(guc_done, 1)

            def down(q, j):
                pe.wait_ge(hh_done, NT * q + j + 1)
                pe.wait_ge(hl_done, NT * q + j + 1)
                if j == 0 and (not isinstance(q, int) or q >= 1):
                    pe.wait_ge(fy_read, q)
                for t in range(TPC):
                    tok = slice(P * t, P * (t + 1))
                    w = slice(2 * D, 3 * D)
                    dst = PS[:, 6 + t // 2, D * (t % 2):D * (t % 2 + 1)]
                    for i, (a, w_) in enumerate(((Hh, WFh), (Hh, WFl), (Hl, WFh))):
                        mm = pe.matmul(dst, a[units(j), j % NH, tok], w_[units(j), j, w], start=j == 0 and i == 0 and t % 2 == 0,
                                       stop=j == NT - 1 and i == 2, skip_group_check=True)
                mm.then_inc(down_done, 1)

            def chunk(q):
                for j in range(NT + 1):
                    if j < NT:
                        gate_up(q, j)
                        gates(q, j, GATE_BANK[j])
                    if j == 0:
                        down(q - 1, NT - 1)
                    if j >= 2:
                        down(q, j - 2)

            def first_gate_up(j):
                pe.wait_ge(wfl_ready, j + 1)
                gate_up(0, j)

            def first_chunk():
                spare = PS[:, 5, :]
                for j in range(NT + 1):
                    if j < NT:
                        if j >= 2:
                            first_gate_up(j)
                        if j == 0:
                            pe.wait_ge(y_added, M)
                            for c in range(2):
                                transpose_gates(0, c, SD[:, c, :])
                            pe.wait_ge(cbT_read, 2)
                            pe.wait_ge(sel_ready, 1)
                            pe.wait_ge(ct_zero, 1)
                        if SPARE_FROM <= j <= SHARED:
                            pe.wait_ge(hid_done, j)
                        gates(0, j, FIRST_GATE_BANK[j])
                    if j >= 2:
                        down(0, j - 2)
                    if 7 <= j < 11:
                        transpose_new_x(1, j - 7, spare, NB // 2 + HB // 2 + j - 7)
                    if j in (11, 12):
                        if j == 12:
                            pe.wait_ge(lt_read, 3)
                        router(1, j - 11, spare)
                    if j == 13:
                        router_by_tokens(1, spare)
                    if j in (15, 16):
                        pe.wait_ge(lg_read, 2)
                        if j == 16:
                            pe.wait_ge(cbT_read, 3)
                        transpose_gates(1, j - 15, spare)

            pe.wait_ge(tanh_done, NU * B * G)
            first_gate_up(0)
            pe.wait_ge(sums_read, M)
            pe.wait_ge(ctx_read, M)
            first_gate_up(1)
            project_out(M - 1, 1, NPROJ + 2 * B * G)
            first_chunk()
            pe.wait_ge(cbT_read, 2 * B)
            with pe.Fori(1, NX) as q:
                chunk(q)
            down(NX - 1, NT - 1)

        @block.scalar
        def _(act):
            def roots(i, t0, blocks):
                act.wait_ge(var_ready, i + 1)
                act.activation(std[:, t0:t0 + blocks], vareps[:, t0:t0 + blocks], ACT.Sqrt).then_inc(std_ready, 1)

            def normalised(i, t0, src, dst, signal):
                act.wait_ge(ln_ready, i + 1)
                for t in range(TPC):
                    b = t0 + t
                    act.activation(dst(t), src(t), ACT.Identity, bias=nbias[:, b:b + 1], scale=rstd[:, b:b + 1]
                                   ).then_inc(signal, 1)

            def expert_weights(j):
                act.wait_ge(wf_in[j % 2], 16 * (j // 2 + 1))
                act.copy(WFh[:, j, :], WFr[:, j % 2, :]).then_inc(wfh_ready, 1)

            def transposed(i, bank):
                act.wait_ge(xt_psum, i + 1)
                act.copy(XTh[:, :, 2 * P * i % TOK:2 * P * i % TOK + 2 * P], bank.rearrange("p (k t) -> p k t", k=KT)
                         ).then_inc(xt_high, 1)

            def value_rows(t):
                act.wait_ge(v_psum, t + 1)
                act.copy(V[:, t], PS[:, 2 + t % 2, :].rearrange("p (g d) -> p g d", g=G)).then_inc(v_ready, 1)

            def rotated(i):
                act.wait_ge(eo_ready, i + 1)
                for s, v in staging_free(i):
                    act.wait_ge(s, v)
                act.copy(staging(i)[:, 0:2, :], EO[i % 2][:]).then_inc(rope_high, 1)

            def staging_free(i):
                if i in (0, 1, 6, 7):
                    return []
                if i < 6:
                    return [(k_stored[i % 2], 16 * (i // 2))]
                return [(qs_in[p], QT) for p in range(2)]

            def x_normalised(i):
                block_of = lambda t: X[:, TPC * i + t, :]
                normalised(i, TPC * i, block_of, block_of, xn_ready)

            def weights_high(w):
                act.wait_ge(kv_in[w], 16)
                act.copy(Wh[:, w], Wr[:, w]).then_inc(high_ready[w], 1)

            roots(0, 0, TPC)
            x_normalised(0)
            weights_high(0)
            roots(1, TPC, TPC)
            transposed(0, PS[:, 0, :])
            transposed(1, PS[:, 1, :])
            weights_high(1)
            x_normalised(1)
            roots(2, 2 * TPC, TPC)
            for i in range(4):
                if i < 3:
                    transposed(2 * i + 2, PS[:, 0, :])
                    transposed(2 * i + 3, PS[:, 1, :])
                if i < 2:
                    x_normalised(i + 2)
                value_rows(2 * i)
                if i < 1:
                    roots(3, 3 * TPC, TPC)
                value_rows(2 * i + 1)
                rotated(i)
            act.wait_ge(al_in, 16)
            act.copy(ALh[:], ALr[:]).then_inc(al_ready, 1)
            for i in range(4, 9):
                if i < 8:
                    rotated(i)
                for t in VALUES_AFTER[i]:
                    value_rows(t)

            def capped(n, u):
                U = NU * n + u
                act.wait_ge(qk_done, U + 1)
                if not isinstance(U, int) or U >= NP:
                    act.wait_ge(pv_done, U - NP + 1)
                w = WIDTH[u % PU]
                act.activation(PR[:, u % NP, 0:w], SC[:, u % 2, 0:w], ACT.Tanh, scale=1.0 / (CAP * DH ** 0.5)
                               ).then_inc(tanh_done, 1)

            CONTEXT_COPIED = {2: -1, 5: 0, 12: 1, 15: 2}

            def context_copied(n, c):
                m = 4 * n + c
                act.wait_ge(pv_done, NU * n + (0, 3, 10, 13)[c + 1])
                if not isinstance(m, int) or m >= 1:
                    act.wait_ge(split_done, m)
                else:
                    act.wait_ge(rope_done, NPRE)
                for h in range(2):
                    head = slice(DH * h, DH * (h + 1))
                    copied = act.copy(CX[head], PV[head, h, :])
                copied.then_inc(ctx_read, 1)

            def exponential(n, u):
                act.wait_ge(tanh_done, NU * n + u + 1)
                w = WIDTH[u % PU]
                act.activation(PR[:, u % NP, 0:w], PR[:, u % NP, 0:w], ACT.Exp, scale=CAP).then_inc(exp_done, 1)

            def body(g, first=False, last=False):
                for b in range(B):
                    n = 2 * g + b
                    for u in range(NU):
                        if u in CONTEXT_COPIED and not (u == 2 and first and b == 0):
                            context_copied(n, CONTEXT_COPIED[u])
                        if u + 1 < NU:
                            capped(n, u + 1)
                        elif not (last and b == B - 1):
                            capped(n + 1, 0)
                        exponential(n, u)
                        if first and b == 0 and u in (2, 3):
                            rotated(6 + u)
                        if last and b == B - 1:
                            if u == 8:
                                roots(NX, 0, HB)
                            if u == 11:
                                act.wait_ge(sel_in, 16)
                                act.wait_ge(sel_zero, 1)
                                act.copy(SL[0:2 * NG, :], SLr[0:2 * NG, :]).then_inc(sel_ready, 1)
                            if u in (12, 13):
                                expert_weights(u - 12)
                            if u == 15:
                                roots(NX + 1, 0, HB)
                            if u in (18, 19):
                                for i in range(2):
                                    transposed(NB // 2 + 2 * (u - 18) + i, SD[:, i, :])

            capped(0, 0)
            body(0, first=True)
            with act.Fori(1, G - 1) as g:
                body(g)
            body(G - 1, last=True)

            def router_products(b, c, bank):
                act.wait_ge(lt_done, 2 * b + c + 1)
                act.copy(LT[b][:, CH * c:CH * (c + 1)], bank[0:NG, :]).then_inc(lt_read, 1)

            def gate_exponentials(b):
                act.wait_ge(gap_ready, 2 * b + 2)
                act.activation(ex[:], ex[:], ACT.Exp).then_inc(e2_ready, 1)

            router_products(0, 0, SD[:, 1, :])
            router_products(0, 1, SD[:, 0, :])
            context_copied(B * G, -1)
            gate_exponentials(0)
            act.wait_ge(y_done, M)

            def hidden(n, j, started):
                act.wait_ge(guc_done, n + 1)
                if started or j >= 2:
                    act.wait_ge(hid_done, n - (j > 0))
                act.activation(sg[units(j), j % 2, :], PS[units(j), 3 * (j % 2), :], ACT.Silu).then_inc(silu_done, 1)
                if not started and j == 1:
                    roots(NX + 2, HB, HB)
                if not started and j == 5:
                    roots(NX + 3, HB, HB)
                act.wait_ge(hid_done, n + 1)
                if started or j >= NH:
                    act.wait_ge(down_done, n - (1 if j < 2 else 2))
                    act.wait_ge(hl_done, n - (1 if j < 2 else 2))
                act.copy(Hh[units(j), j % NH, :], hd[units(j), j % 2, :]).then_inc(hh_done, 1)

            def chunk(q, first=False):
                for j in range(NT):
                    if first and j + 2 < NT:
                        expert_weights(j + 2)
                    hidden(NT * q + j, j, not first)
                    if first:
                        spare = PS[:, 5, :]
                        if 7 <= j < 11:
                            transposed(NB // 2 + HB // 2 + j - 7, spare)
                        if j in (11, 12):
                            router_products(1, j - 11, spare)
                        if j == 14:
                            gate_exponentials(1)
                    else:
                        if j == 0:
                            act.wait_ge(down_done, NT * q)
                            act.copy(Y, FY).then_inc(fy_read, 1)
                        if j == 2:
                            roots(2 * NX + q - 1, 0, TPC)
                        if j == 4:
                            output_norm(q - 1, Y)

            def output_norm(q, src):
                if not isinstance(q, int) or q >= 1:
                    act.wait_ge(o_out, 32 * q)
                normalised(2 * NX + q, 0, lambda t: src[:, t, :], lambda t: O[:, t, :], fn_ready)

            chunk(0, first=True)
            with act.Fori(1, NX) as q:
                chunk(q)
            roots(3 * NX - 1, 0, TPC)
            output_norm(NX - 1, FY)

        @block.gpsimd
        def _(pool):
            own = Steps(pool, pool_step)
            pool.memset(VS[0][:], 1.0).then_inc(v_ones[0], 1)
            for w in range(2):
                pool.wait_ge(high_ready[w], 1)
                pool.tensor_tensor(Wl[:, w], Wr[:, w], Wh[:, w].bitcast(F32), ALU.subtract).then_inc(low_ready[w], 1)

            def split(raw, hi, lo, ready):
                own.add(pool.tensor_copy(hi[:], raw[:]))
                own.wait()
                pool.tensor_tensor(lo[:], raw[:], hi[:].bitcast(F32), ALU.subtract).then_inc(ready, 1)

            def expert_weights_low(j):
                pool.wait_ge(wfh_ready, j + 1)
                pool.tensor_tensor(WFl[:, j, :], WFr[:, j % 2, :], WFh[:, j, :].bitcast(F32), ALU.subtract
                                   ).then_inc(wfl_ready, 1)

            pool.wait_ge(q_in, 16)
            split(WQr, WQh, WQl, wq_ready)

            def rotated_low(i):
                pool.wait_ge(rope_high, i + 1)
                pool.tensor_tensor(staging(i)[:, 2:4, :], EO[i % 2][:], staging(i)[:, 0:2, :].bitcast(F32), ALU.subtract
                                   ).then_inc(rope_done, 1)

            for i in range(8):
                rotated_low(i)

            def body(g, first=False, last=False):
                for b in range(B):
                    n = 2 * g + b
                    for u in range(NU):
                        p, v = divmod(u, PU)
                        if v not in MASKED:
                            continue
                        wait_apart(pool, exp_done, NU * n + u + 1, pool_passed)
                        if v in CHUNK_END:
                            spots = [PR[:, u % NP, 0:CH].rearrange("p (a s) -> p a s", a=2)[:, :, 0:P]]
                        else:
                            spots = [PR[:, u % NP, 0:P].unsqueeze(1),
                                     PR[:, u % NP, CH:CH + 2 * P].rearrange("p (a s) -> p a s", a=2)]
                        for spot in spots:
                            done = pool.affine_select(out=spot, in_=spot, compare_op=ALU.is_ge, fill=0.0, base=0,
                                                      pattern=[[0, spot.shape[1]], [1, P]], channel_multiplier=-1)
                        done.then_inc(mask_done, 1)
                        if first and b == 0 and u == 2:
                            rotated_low(8)
                            rotated_low(9)
                        if first and b == 0 and u == 5:
                            pool.wait_ge(ks1_stored, 16)
                            pool.memset(VS[1][:], 1.0).then_inc(v_ones[1], 1)
                        if u == 5 and b == 0:
                            if not isinstance(g, int) or g >= 1:
                                wait_apart(pool, y_done, 8 * g, pool_passed)
                            wait_apart(pool, o_in, 16 * (g + 1), pool_passed)
                            split(WOr, WOh, WOl, wo_ready)
                        if u == PU + 5 and b == 0 and not last:
                            wait_apart(pool, q_in, 16 * (g + 2), pool_passed)
                            wait_apart(pool, proj_done, NPROJ + 4 * g + 4, pool_passed)
                            split(WQr, WQh, WQl, wq_ready)
                        if last and b == B - 1:
                            if u == 2:
                                for i in range(2):
                                    pool.wait_ge(qs_in[i], QT * B * G)
                                pool.memset(SL[:].bitcast(F32), 0.0).then_inc(sel_zero, 1)
                            if u == PU + 5:
                                pool.wait_ge(sel_ready, 1)
                                pool.memset(CT[:].bitcast(F32), 0.0).then_inc(ct_zero, 1)
                                expert_weights_low(0)
                                expert_weights_low(1)
                            if u == 5:
                                pool.wait_ge(r_in, 16)
                                split(Rr, Rh, Rl, rw_ready)

            body(0, first=True)
            per = own.k - 1
            with pool.Fori(1, G - 1) as g:
                own.base, own.k = 1 + per * g, 0
                body(g)
            own.base, own.k = 1 + per * (G - 1), 0
            body(G - 1, last=True)
            pool.wait_ge(y_added, M)
            for j in range(2, NT):
                expert_weights_low(j)

        @block.vector
        def _(dve):
            own = Steps(dve, dve_step)

            def ln_stats(src, t0, blocks):
                c = slice(t0, t0 + blocks)
                for t in range(blocks):
                    own.add(dve.bn_stats(stats[:, t0 + t, :], src(t)))
                own.wait_apart(dve_passed)
                for t in range(blocks):
                    own.add(dve.bn_aggr(mv[:, t0 + t, :], stats[:, t0 + t, :]))
                own.wait()
                dve.tensor_scalar(vareps[:, c], mv[:, c, 1], EPS, None, ALU.add).then_inc(var_ready, 1)

            def ln_factors(i, t0, blocks):
                c = slice(t0, t0 + blocks)
                dve.wait_ge(std_ready, i + 1)
                own.add(dve.reciprocal(rstd[:, c], std[:, c]))
                own.wait()
                own.add(dve.tensor_tensor(newton[:, c], rstd[:, c], rstd[:, c], ALU.mult))
                own.wait()
                own.add(dve.tensor_tensor(newton[:, c], newton[:, c], vareps[:, c], ALU.mult))
                own.wait()
                own.add(dve.tensor_scalar(newton[:, c], newton[:, c], -0.5, 1.5, ALU.mult, ALU.add))
                own.wait()
                own.add(dve.tensor_tensor(rstd[:, c], rstd[:, c], newton[:, c], ALU.mult))
                own.wait()
                dve.scalar_tensor_tensor(out=nbias[:, c], in0=mv[:, c, 0], scalar=-1.0, in1=rstd[:, c],
                                         op0=ALU.mult, op1=ALU.mult).then_inc(ln_ready, 1)

            def transposed(i, bank):
                dve.wait_ge(xt_high, i + 1)
                at = slice(2 * P * i % TOK, 2 * P * i % TOK + 2 * P)
                dve.tensor_tensor(XTl[:, :, at], bank.rearrange("p (k t) -> p k t", k=KT),
                                  XTh[:, :, at].bitcast(F32), ALU.subtract).then_inc(xt_low, 1)

            def ln_stats_x(i):
                dve.wait_ge(x_in[i], 16)
                ln_stats(lambda t: X[:, TPC * i + t, :], TPC * i, TPC)

            halves = [slice(0, CH), slice(CH, 2 * CH)]

            def rope_products(i, c, buffer_waits):
                def table(k):
                    return CS[:, k:k + 1, halves[c]].broadcast_to([P, 2, CH])

                dve.wait_ge(proj_done, i + 1)
                for sem_, v in buffer_waits:
                    dve.wait_ge(sem_, v)
                own.add(dve.tensor_tensor(EO[rotated_in(i)][:], side_banks(i), table(0), ALU.mult))
                dve.tensor_tensor(ts[:], side_banks(i), table(1), ALU.mult).then_inc(proj_read, 1)

            def rope_sums(i):
                eo = EO[rotated_in(i)]
                dve.wait_ge(proj_read, i + 1)
                own.wait()
                own.add(dve.tensor_tensor(eo[:, 0, :], eo[:, 0, :], ts[:, 1, :], ALU.subtract))
                return dve.tensor_tensor(eo[:, 1, :], eo[:, 1, :], ts[:, 0, :], ALU.add)

            def rope_parts(i, c, stage_waits=()):
                eo = EO[rotated_in(i)]
                own.add(rope_sums(i))
                own.wait()
                for sem_, v in stage_waits:
                    dve.wait_ge(sem_, v)
                own.add(dve.tensor_copy(ST[:, 0:2, halves[c]], eo[:]))
                own.wait()
                dve.tensor_tensor(ST[:, 2:4, halves[c]], eo[:], ST[:, 0:2, halves[c]].bitcast(F32), ALU.subtract
                                  ).then_inc(rope_done, 1)

            def rotation_products(i):
                rope_products(i, i % 2, ([(rope_done, i - 1)] if i >= 2 else []) + ([(eo_ready, i)] if i else []))

            def rotation_sums(i):
                rope_sums(i).then_inc(eo_ready, 1)

            ln_stats_x(0)
            ln_factors(0, 0, TPC)
            ln_stats_x(1)
            transposed(0, PS[:, 0, :])
            transposed(1, PS[:, 1, :])
            ln_factors(1, TPC, TPC)
            ln_stats_x(2)
            dve.wait_ge(cs_in, 16)
            for i in range(NPRE):
                rotation_products(i)
                if i < 3:
                    transposed(2 * i + 2, PS[:, 0, :])
                    transposed(2 * i + 3, PS[:, 1, :])
                if i < 2:
                    ln_factors(i + 2, TPC * (i + 2), TPC)
                if i == 0:
                    ln_stats_x(3)
                rotation_sums(i)
            dve.wait_ge(bo_in, 16)

            def row_sums(n, p, c):
                dve.wait_ge(pv_done, NU * n + PU * p + (3, PU)[c])
                m = 4 * n + 2 * p + c
                if not isinstance(m, int) or m >= 1:
                    dve.wait_ge(split_done, m)
                own.add(dve.tensor_copy(RS[0:DH], PV[DH:2 * DH, 0, :]))
                own.add(dve.tensor_copy(RS[DH:2 * DH], PV[0:DH, 1, :]))
                own.wait()
                dve.sem_inc(sums_read, 1)

            def normalise(m):
                own.add(dve.reciprocal(RS, RS))
                own.wait()
                dve.wait_ge(ctx_read, m + 1)
                own.add(dve.tensor_tensor(CX, CX, RS, ALU.mult))
                own.wait()
                if not isinstance(m, int) or m >= 1:
                    dve.wait_ge(y_done, m)
                src = CX.rearrange("p (t s) -> p t s", t=TPC)
                own.add(dve.tensor_copy(CTh[:], src))
                own.wait()
                dve.tensor_tensor(CTl[:], src, CTh[:].bitcast(F32), ALU.subtract).then_inc(split_done, 1)

            def add_out(m, b, c):
                dve.wait_ge(y_done, m + 1)
                t = NB // B * b + TPC * c
                acc = yacc[:, t:t + TPC, :]
                dve.tensor_tensor(acc, FY, acc, ALU.add).then_inc(y_added, 1)

            def attention_stats(b):
                dve.wait_ge(y_added, M - 4 * (B - 1 - b))
                ln_stats(lambda t: yacc[:, HB * b + t, :], HB * b, HB)

            def blocks_normalised(b, src, blocks, signal=None):
                for t in blocks:
                    c = HB * b + t
                    done = dve.tensor_scalar(yacc[:, c, :], src[:, c, :], rstd[:, c:c + 1], nbias[:, c:c + 1],
                                             ALU.mult, ALU.add)
                    if signal is None:
                        own.add(done)
                    else:
                        done.then_inc(signal, 1)

            def attention_norm(b, half):
                if half == 0:
                    ln_factors(NX + 2 * b, HB * b, HB)
                    dve.wait_ge(ln_ready, NX + 2 * b + 1)
                blocks_normalised(b, yacc, range(4 * half, 4 * half + 4))

            def new_x(b):
                c = slice(HB * b, HB * (b + 1))
                dve.wait_ge(x2_in[b], 16)
                own.wait()
                own.add(dve.tensor_tensor(X2[:, c, :], X2[:, c, :], yacc[:, c, :], ALU.add))

            def new_x_stats(b):
                dve.wait_ge(dve_step, own.base + own.k)
                ln_stats(lambda t: X2[:, HB * b + t, :], HB * b, HB)

            def new_x_norm(b, half):
                if half == 0:
                    ln_factors(NX + 2 * b + 1, HB * b, HB)
                    dve.wait_ge(ln_ready, NX + 2 * b + 2)
                blocks_normalised(b, X2, range(4 * half, 4 * half + 4), xn_ready)

            def router_read(b, bank):
                dve.wait_ge(lg_done, b + 1)
                dve.tensor_copy(LG[:], bank[:, 0:16 * HB].rearrange("p (t r) -> p t r", r=16)[:, :, 0:NG]).then_inc(lg_read, 1)

            def two_best(b):
                dve.wait_ge(lg_read, b + 1)
                dve.tensor_scalar(ex[:, 1, :], LG[:, :, NE], -1.0, None, ALU.mult).then_inc(gap_ready, 1)
                for t in range(HB):
                    own.add(dve.max(top[:, t, :], LG[:, t, 0:NE]))
                own.wait()
                dve.tensor_tensor(ex[:, 0, :], top[:, :, 1], top[:, :, 0], ALU.subtract).then_inc(gap_ready, 1)
                for t in range(HB):
                    own.add(dve.max_index(topi[:, t, :], top[:, t, :], LG[:, t, 0:NE]))
                own.wait()
                own.add(dve.tensor_copy(topf[:], topi[:]))

            def weigh(b):
                dve.wait_ge(e2_ready, b + 1)
                own.add(dve.tensor_scalar(den[:], ex[:], 1.0, None, ALU.add))
                own.wait()
                own.add(dve.reciprocal(wt[:, 0:2, :], den[:]))
                own.wait()
                own.add(dve.tensor_tensor(wt[:, 2, :], ex[:, 0, :], wt[:, 0, :], ALU.mult))
                own.wait()
                for e in range(NE):
                    own.add(dve.scalar_tensor_tensor(out=CB[:, :, e], in0=topf[:, :, 0], scalar=float(e),
                                                     in1=wt[:, 0, :], op0=ALU.is_equal, op1=ALU.mult))
                    own.add(dve.scalar_tensor_tensor(out=CB2[:, :, e], in0=topf[:, :, 1], scalar=float(e),
                                                     in1=wt[:, 2, :], op0=ALU.is_equal, op1=ALU.mult))
                own.wait()
                own.add(dve.tensor_tensor(CB[:, :, 0:NE], CB[:, :, 0:NE], CB2[:, :, 0:NE], ALU.add))
                own.add(dve.tensor_copy(CB[:, :, NE], wt[:, 1, :]))
                own.wait()
                own.add(dve.tensor_copy(CBh[:], CB[:]))
                own.wait()
                if b > 0:
                    dve.wait_ge(cbT_done, 2 * b)
                dve.tensor_copy(CBx[:, :, 0:NG], CBh[:].bitcast(F32)).then_inc(cb_ready, 1)
                dve.tensor_tensor(CBx[:, :, NG:2 * NG], CB[:], CBh[:].bitcast(F32), ALU.subtract).then_inc(cb_ready, 1)

            def gates_read(b, c, bank):
                i = 2 * b + c
                dve.wait_ge(ct_zero, 1)
                dve.wait_ge(cbT_done, i + 1)
                dve.tensor_copy(CT[0:2 * NG, CH * i:CH * (i + 1)], bank[0:2 * NG, :]).then_inc(cbT_read, 1)

            def body(g, first=False, last=False):
                for b in range(B):
                    n = 2 * g + b
                    more = not (last and b == B - 1)
                    for p in range(2):
                        m = 4 * n + 2 * p
                        early = not more
                        before = not (first and b == 0 and p == 0)
                        if early and p == 1:
                            new_x_stats(0)
                        if before:
                            normalise(m - 1)
                            add_out(m - 2, b if p == 1 else 1 - b, 0)
                        else:
                            dve.wait_ge(rope_done, NPRE)
                            dve.wait_ge(ks1_stored, 16)
                        row_sums(n, p, 0)
                        if before:
                            add_out(m - 1, b if p == 1 else 1 - b, 1)
                        if early and p == 0:
                            attention_stats(0)
                        if early and p == 1:
                            for half in range(2):
                                new_x_norm(0, half)
                        normalise(m)
                        if more and p == 0:
                            rope_products(NPROJ + 2 * n + 2, 0, [(rope_done, NPROJ + 2 * n + 2)])
                            rope_parts(NPROJ + 2 * n + 2, 0, [(qs_in[i], QT * (n + 1)) for i in range(2)]
                                       + ([(last_k_stored, 16 * 3)] if first and b == 0 else []))
                            rope_products(NPROJ + 2 * n + 3, 1, [(rope_done, NPROJ + 2 * n + 3)])
                            rope_parts(NPROJ + 2 * n + 3, 1)
                        if early and p == 0:
                            attention_norm(0, 0)
                            attention_norm(0, 1)
                            new_x(0)
                        if early and p == 1:
                            for i in range(HB // 2):
                                transposed(NB // 2 + i, SD[:, i % 2, :])
                        row_sums(n, p, 1)
                        if early and p == 1:
                            router_read(0, SD[:, 0, :])

            steps = B * (2 * 4 + 4 * 5)
            body(0, first=True)
            begun = own.base + own.k
            with dve.Fori(1, G - 1) as g:
                own.base, own.k = begun + steps * (g - 1), 0
                body(g)
                assert own.k == steps
            own.base, own.k = begun + steps * (G - 2), 0
            body(G - 1, last=True)
            two_best(0)
            normalise(M - 1)
            add_out(M - 2, 1, 0)
            weigh(0)
            add_out(M - 1, 1, 1)
            for c in range(2):
                gates_read(0, c, SD[:, c, :])

            def hidden(n, j, gate_bank, started):
                dve.wait_ge(silu_done, n + 1)
                if started or j >= 2:
                    dve.wait_ge(hh_done, n - (j > 0))
                    dve.wait_ge(hl_done, n - (j > 0))
                h = hd[units(j), j % 2, :]
                up = PS[TAIL:P, 3 * (j % 2), :] if j == NT - 1 else PS[:, 3 * (j % 2) + 1, :]
                own.add(dve.tensor_tensor(h, up, sg[units(j), j % 2, :], ALU.mult))
                own.wait()
                dve.tensor_tensor(h, PS[units(j), gate_bank, :], h, ALU.mult).then_inc(hid_done, 1)

            def hidden_low(n, j, started):
                dve.wait_ge(hh_done, n + 1)
                if started or j >= NH:
                    dve.wait_ge(down_done, n - (1 if j < 2 else 2))
                dve.tensor_tensor(Hl[units(j), j % NH, :], hd[units(j), j % 2, :],
                                  Hh[units(j), j % NH, :].bitcast(F32), ALU.subtract
                                  ).then_inc(hl_done, 1)

            def first_chunk():
                spare = PS[:, 5, :]
                for j in range(NT):
                    hidden(j, j, FIRST_GATE_BANK[j], False)
                    if j == 0:
                        attention_stats(1)
                    if j in (1, 2):
                        attention_norm(1, j - 1)
                    if j == 3:
                        new_x(1)
                    if j == 4:
                        new_x_stats(1)
                    if j in (5, 6):
                        new_x_norm(1, j - 5)
                    if 7 <= j < 11:
                        transposed(NB // 2 + HB // 2 + j - 7, spare)
                    if j == 13:
                        router_read(1, spare)
                        two_best(1)
                    if j == 14:
                        weigh(1)
                    if j in (15, 16):
                        gates_read(1, j - 15, spare)
                    hidden_low(j, j, False)

            def chunk(q):
                for j in range(NT):
                    n = NT * q + j
                    hidden(n, j, GATE_BANK[j], True)
                    if j == 1:
                        dve.wait_ge(fy_read, q)
                        ln_stats(lambda t: Y[:, t, :], 0, TPC)
                    if j == 3:
                        ln_factors(2 * NX + q - 1, 0, TPC)
                    if j == 5:
                        residual(q - 1)
                    hidden_low(n, j, True)

            def residual(q):
                for h in range(2):
                    dve.wait_ge(fn_ready, TPC * q + TPC // 2 * (h + 1))
                    half = O[:, TPC // 2 * h:TPC // 2 * (h + 1), :]
                    dve.tensor_tensor(half, half, X2[:, bass.ds(TPC * q + TPC // 2 * h, TPC // 2), :], ALU.add
                                      ).then_inc(o_ready, 1)

            steps = NT + 2 * TPC + 5
            first_chunk()
            begun = own.base + own.k
            with dve.Fori(1, NX) as q:
                own.base, own.k = begun + steps * (q - 1), 0
                chunk(q)
                assert own.k == steps, own.k
            own.base, own.k = begun + steps * (NX - 1), 0
            dve.wait_ge(down_done, NT * NX)
            ln_stats(lambda t: FY[:, t, :], 0, TPC)
            ln_factors(3 * NX - 1, 0, TPC)
            residual(NX - 1)




def _tables():
    inv = (1.0 / 10000.0 ** (np.arange(0, DH, 2, dtype=np.float32) / DH)).astype(np.float32)
    angle = np.arange(S, dtype=np.float32)[None, :] * inv[:, None]
    cs = np.stack([np.tile(np.cos(angle), (4, 1)), np.tile(np.sin(angle), (4, 1))], 1).astype(np.float32)

    def part(v):
        m, e = np.frexp(v)
        return np.ldexp(np.round(m * 4096) / 4096, e)

    pos = np.arange(S, dtype=np.float64)
    al = np.zeros((G * 4 + R * 4, S))
    for g in range(G):
        al[4 * g:4 * g + 2] = pos * 2.0 ** -g
        al[4 * g + 2:4 * g + 4] = 2.0 ** -g
    for h in range(R):
        slope = 2.0 ** (-(h + 1) * 8.0 / H)
        rows = []
        for v in (np.full(S, slope), -slope * pos):
            rows += [part(v), part(v - part(v))]
        al[4 * G + 4 * h:4 * G + 4 * h + 4] = rows
    sel = np.zeros((2 * NG, NT * P), np.float32)
    for i in range(HID):
        e = min(i // IM, NE)
        sel[e, i] = sel[NG + e, i] = 1.0
    return cs, al.astype(np.float32), np.eye(P, dtype=np.float32), sel


def kernel(**inputs):
    import concourse.bacc as _bacc
    from concourse.bass_utils import run_bass_kernel_spmd as _run

    a = {k[3:]: np.asarray(v) for k, v in inputs.items()}
    cs, al, ident, sel = _tables()
    x = a["attn_hidden_states"].reshape(TOK, D)
    wq = a["attn_Wq"].reshape(KT, P, G, R, 32, 2).transpose(2, 1, 0, 5, 3, 4).reshape(G, P, KT, 2, P)
    wk = a["attn_Wk"].reshape(KT, P, 2, 4, 32, 2).transpose(1, 0, 2, 5, 3, 4).reshape(P, KT, CH)
    wv = a["attn_Wv"].reshape(KT, P, CH).transpose(1, 0, 2)
    wo = a["attn_Wo"].reshape(G, 2, P, D).transpose(0, 2, 1, 3)
    gu, dn = a["ffn_gate_up_proj"], a["ffn_down_proj"]
    pad = np.zeros((NT * P - HID, D), np.float32)
    gate = np.concatenate([gu[:, :IM].reshape(NE * IM, D), a["ffn_sh_gate_w"], pad])
    up = np.concatenate([gu[:, IM:].reshape(NE * IM, D), a["ffn_sh_up_w"], pad])
    down = np.concatenate([dn.transpose(0, 2, 1).reshape(NE * IM, D), a["ffn_sh_down_w"].T, pad])
    gate[-TAIL:] = up[(NT - 1) * P:HID]
    tiles = [w.reshape(NT, P, KT, P).transpose(0, 3, 2, 1).reshape(NT, P, D) for w in (gate, up)]
    wf = np.concatenate([*tiles, down.reshape(NT, P, D)], axis=2)
    wr = np.concatenate([a["ffn_router_weight"], a["ffn_shared_gate_w"], np.zeros((P - NG, D), np.float32)])
    wr = wr.reshape(P, KT, P).transpose(2, 1, 0)

    nc = _bacc.Bacc("TRN2", target_bir_lowering=False, num_devices=1)
    arrays, args = {}, []
    for name, v in dict(x=x, wq=wq, wk=wk, wv=wv, wo=wo, bo=a["attn_bo"], wf=wf, wr=wr, cs=cs, al=al,
                        ident=ident, sel=sel).items():
        v = np.ascontiguousarray(v)
        arrays[f"in_{name}"] = v
        args.append(nc.dram_tensor(f"in_{name}", v.shape, mybir.dt.from_np(v.dtype), kind="ExternalInput").ap())
    args.append(nc.dram_tensor("out_0", (TOK, D), F32, kind="ExternalOutput").ap())
    build(nc, *args)
    r = _run(nc, [arrays], core_ids=[0])
    return r.results[0]["out_0"].reshape(B, S, D)
```
